# Optimizing a Trainium2 kernel written in Bass

```python
import numpy as np
import jax
import jax.numpy as jnp

def _softmax(x, axis=-1):
    return jax.nn.softmax(x, axis=axis)

def _gelu(x):
    return jax.nn.gelu(x, approximate=True)

def _silu(x):
    return jax.nn.silu(x)

def _sigmoid(x):
    return jax.nn.sigmoid(x)

def _layernorm(x, axis=-1, eps=1e-05):
    m = jnp.mean(x, axis=axis, keepdims=True)
    v = jnp.var(x, axis=axis, keepdims=True)
    return (x - m) / jnp.sqrt(v + eps)

def _scatter_add(tgt, idx, src, axis=0):
    return tgt.at[idx].add(src)

def _segment_sum(src, seg, n):
    return jax.ops.segment_sum(src, seg, n)
kernel_name = 'mk_decoder_preln_d1_seqx_r4_519144'

def setup_inputs(seed: int=0):
    np.random.seed(seed)
    _w = jnp.asarray

    def _rec_inputs():
        import jax
        import jax.numpy as jnp
        _rk = jax.random.key(seed)
        x = -7.109e-05 + 0.9999 * jax.random.normal(jax.random.fold_in(_rk, 1), (4, 1024, 256), jnp.float32)
        _lenS = 1024 - jax.random.randint(jax.random.fold_in(_rk, 7), (4,), 0, max(1, 1024 // 4) + 1, jnp.int32)
        _lenS2 = 77 - jax.random.randint(jax.random.fold_in(_rk, 8), (4,), 0, max(1, 77 // 4) + 1, jnp.int32)
        _ctx_768P = jax.random.normal(jax.random.fold_in(_rk, 11), (4, 16, 192), jnp.float32)
        _ctx_768c = jax.random.dirichlet(jax.random.fold_in(_rk, 511), 0.3 * jnp.ones((16,), jnp.float32), (4, 77))
        _ctx_768t = jnp.einsum('bsk,bkd->bsd', _ctx_768c, _ctx_768P)
        _ctx_768t = _ctx_768t * jax.lax.rsqrt(jnp.mean(jnp.square(_ctx_768t)) + 1e-12) * 0.953939
        ctx_768 = 0.000486113 + 1.00014 * (_ctx_768t + 0.3 * jax.random.normal(jax.random.fold_in(_rk, 611), (4, 77, 192), jnp.float32))
        return (x, ctx_768)
    x, ctx_768 = _rec_inputs()

    def _L0_attn_setup():
        import jax, jax.numpy as jnp
        import numpy as np
        NUM_HEADS = 16
        CURVATURE = 1.0

        def _split_heads(t, H):
            B, N, D = t.shape
            return t.reshape(B, N, H, D // H).transpose(0, 2, 1, 3)
        key = jax.random.key(seed)
        ks = jax.random.split(key, 5)
        B, N, D = (2, 512, 256)
        x = jax.random.normal(ks[0], (B, N, D), dtype=jnp.float32) * 0.02
        s = 1.0 / np.sqrt(D)
        wq = jax.random.normal(ks[1], (D, D), dtype=jnp.float32) * s
        wk = jax.random.normal(ks[2], (D, D), dtype=jnp.float32) * s
        wv = jax.random.normal(ks[3], (D, D), dtype=jnp.float32) * s
        wo = jax.random.normal(ks[4], (D, D), dtype=jnp.float32) * s
        return {'x': x, 'wq': wq, 'wk': wk, 'wv': wv, 'wo': wo}
    _L0_attn_all = _L0_attn_setup()
    _L0_attn_in = {k: v for k, v in _L0_attn_all.items() if k in ('wq', 'wk', 'wv', 'wo')}
    del _L0_attn_all

    def _L0_xattn_setup():
        import jax, jax.numpy as jnp
        import numpy as np
        HEADS = 16
        DIM_HEAD = 64
        key = jax.random.key(seed)
        ks = jax.random.split(key, 8)
        B, S, D = (16, 1024, 256)
        K, DE = (77, 192)
        inner = HEADS * DIM_HEAD
        hidden_states = jax.random.normal(ks[0], (B, S, D), dtype=jnp.float32)
        encoder_hidden_states = jax.random.normal(ks[1], (B, K, DE), dtype=jnp.float32)
        sc_q = 1.0 / np.sqrt(D)
        sc_kv = 1.0 / np.sqrt(DE)
        sc_o = 1.0 / np.sqrt(inner)
        Wq = jax.random.normal(ks[2], (D, inner), dtype=jnp.float32) * sc_q
        Wk = jax.random.normal(ks[3], (DE, inner), dtype=jnp.float32) * sc_kv
        Wv = jax.random.normal(ks[4], (DE, inner), dtype=jnp.float32) * sc_kv
        Wo = jax.random.normal(ks[5], (inner, D), dtype=jnp.float32) * sc_o
        bo = jax.random.normal(ks[6], (D,), dtype=jnp.float32) * 0.01
        return {'hidden_states': hidden_states, 'encoder_hidden_states': encoder_hidden_states, 'Wq': Wq, 'Wk': Wk, 'Wv': Wv, 'Wo': Wo, 'bo': bo}
    _L0_xattn_all = _L0_xattn_setup()
    _L0_xattn_in = {k: v for k, v in _L0_xattn_all.items() if k in ('Wq', 'Wk', 'Wv', 'Wo', 'bo')}
    del _L0_xattn_all

    def _L0_ffn_setup():
        import jax, jax.numpy as jnp
        import numpy as np
        D_MODEL = 256
        D_FF = 1024
        NUM_EXPERTS = 8
        B, N = (16, 256)
        key = jax.random.key(seed)
        ks = jax.random.split(key, 7)
        s_in = 1.0 / np.sqrt(D_MODEL)
        s_ff = 1.0 / np.sqrt(D_FF)
        return {'x': jax.random.normal(ks[0], (B, N, D_MODEL), dtype=jnp.float32), 'Wr': jax.random.uniform(ks[1], (D_MODEL, NUM_EXPERTS), jnp.float32, -s_in, s_in), 'br': jax.random.uniform(ks[2], (NUM_EXPERTS,), jnp.float32, -s_in, s_in), 'W1': jax.random.uniform(ks[3], (NUM_EXPERTS, D_MODEL, D_FF), jnp.float32, -s_in, s_in), 'b1': jax.random.uniform(ks[4], (NUM_EXPERTS, D_FF), jnp.float32, -s_in, s_in), 'W2': jax.random.uniform(ks[5], (NUM_EXPERTS, D_FF, D_MODEL), jnp.float32, -s_ff, s_ff), 'b2': jax.random.uniform(ks[6], (NUM_EXPERTS, D_MODEL), jnp.float32, -s_ff, s_ff)}
    _L0_ffn_all = _L0_ffn_setup()
    _L0_ffn_in = {k: v for k, v in _L0_ffn_all.items() if k in ('Wr', 'br', 'W1', 'b1', 'W2', 'b2')}
    del _L0_ffn_all
    return {'x': x, 'ctx_768': ctx_768, 'L0_attn_wq': _L0_attn_in['wq'], 'L0_attn_wk': _L0_attn_in['wk'], 'L0_attn_wv': _L0_attn_in['wv'], 'L0_attn_wo': _L0_attn_in['wo'], 'L0_xattn_Wq': _L0_xattn_in['Wq'], 'L0_xattn_Wk': _L0_xattn_in['Wk'], 'L0_xattn_Wv': _L0_xattn_in['Wv'], 'L0_xattn_Wo': _L0_xattn_in['Wo'], 'L0_xattn_bo': _L0_xattn_in['bo'], 'L0_ffn_Wr': _L0_ffn_in['Wr'], 'L0_ffn_br': _L0_ffn_in['br'], 'L0_ffn_W1': _L0_ffn_in['W1'], 'L0_ffn_b1': _L0_ffn_in['b1'], 'L0_ffn_W2': _L0_ffn_in['W2'], 'L0_ffn_b2': _L0_ffn_in['b2']}

def reference(x, ctx_768, L0_attn_wq, L0_attn_wk, L0_attn_wv, L0_attn_wo, L0_xattn_Wq, L0_xattn_Wk, L0_xattn_Wv, L0_xattn_Wo, L0_xattn_bo, L0_ffn_Wr, L0_ffn_br, L0_ffn_W1, L0_ffn_b1, L0_ffn_W2, L0_ffn_b2):
    import jax
    import jax.numpy as jnp

    def _L0_attn_ref(x, wq, wk, wv, wo):
        import jax, jax.numpy as jnp
        import numpy as np
        NUM_HEADS = 16
        CURVATURE = 1.0

        def _split_heads(t, H):
            B, N, D = t.shape
            return t.reshape(B, N, H, D // H).transpose(0, 2, 1, 3)
        B, N, D = x.shape
        H = NUM_HEADS
        c = CURVATURE
        q = _split_heads(x @ wq.T, H)
        k = _split_heads(x @ wk.T, H)
        v = _split_heads(x @ wv.T, H)
        q_norm_sq = jnp.sum(q * q, axis=-1, keepdims=True)
        k_norm_sq = jnp.sum(k * k, axis=-1)[:, :, None, :]
        qk = jnp.einsum('bhqd,bhkd->bhqk', q, k)
        diff_sq = jnp.maximum(q_norm_sq + k_norm_sq - 2.0 * qk, 0.0)
        denom = jnp.maximum((1.0 - c * q_norm_sq) * (1.0 - c * k_norm_sq), 1e-06)
        cosh_arg = jnp.maximum(1.0 + 2.0 * c * diff_sq / denom, 1.0)
        distance = jnp.arccosh(cosh_arg)
        attn = jax.nn.softmax(-distance, axis=-1)
        out = jnp.einsum('bhqk,bhkd->bhqd', attn, v)
        out = out.transpose(0, 2, 1, 3).reshape(B, N, D)
        return out @ wo.T

    def _L0_xattn_ref(hidden_states, encoder_hidden_states, Wq, Wk, Wv, Wo, bo):
        import jax, jax.numpy as jnp
        import numpy as np
        HEADS = 16
        DIM_HEAD = 64
        B, S, D = hidden_states.shape
        K = encoder_hidden_states.shape[1]
        H, Dh = (HEADS, DIM_HEAD)
        scale = 1.0 / np.sqrt(Dh)
        q = hidden_states @ Wq
        k = encoder_hidden_states @ Wk
        v = encoder_hidden_states @ Wv
        q = q.reshape(B, S, H, Dh).transpose(0, 2, 1, 3)
        k = k.reshape(B, K, H, Dh).transpose(0, 2, 1, 3)
        v = v.reshape(B, K, H, Dh).transpose(0, 2, 1, 3)
        scores = jnp.einsum('bhsd,bhkd->bhsk', q, k) * scale
        probs = jax.nn.softmax(scores, axis=-1)
        out = jnp.einsum('bhsk,bhkd->bhsd', probs, v)
        out = out.transpose(0, 2, 1, 3).reshape(B, S, H * Dh)
        out = out @ Wo + bo
        return out

    def _L0_ffn_ref(x, Wr, br, W1, b1, W2, b2):
        import jax, jax.numpy as jnp
        import numpy as np
        D_MODEL = 256
        D_FF = 1024
        NUM_EXPERTS = 8
        B, N = (16, 256)
        scores = jnp.einsum('bh,he->be', x.mean(axis=1), Wr) + br
        top1 = jnp.argmax(scores, axis=-1)
        w1 = W1[top1]
        c1 = b1[top1]
        w2 = W2[top1]
        c2 = b2[top1]
        h = jax.nn.relu(jnp.einsum('bnh,bhf->bnf', x, w1) + c1[:, None, :])
        out = jnp.einsum('bnf,bfh->bnh', h, w2) + c2[:, None, :]
        return out
    x = x + _L0_attn_ref(_layernorm(x, axis=-1), L0_attn_wq, L0_attn_wk, L0_attn_wv, L0_attn_wo)
    x = x + _L0_xattn_ref(_layernorm(x, axis=-1), ctx_768, L0_xattn_Wq, L0_xattn_Wk, L0_xattn_Wv, L0_xattn_Wo, L0_xattn_bo)
    x = x + _L0_ffn_ref(_layernorm(x, axis=-1), L0_ffn_Wr, L0_ffn_br, L0_ffn_W1, L0_ffn_b1, L0_ffn_W2, L0_ffn_b2)
    return x

_drawn_inputs = setup_inputs


def setup_inputs(seed=0):
    import zlib

    import numpy as np

    out = dict(_drawn_inputs(seed))
    spreads = {}
    factors = {'L0_attn_wq': 8.0,
     'L0_attn_wk': 8.0,
     'L0_xattn_bo': 6.198,
     'L0_ffn_b1': 4.515,
     'L0_ffn_b2': 3.523}
    for name, (base, spread) in spreads.items():
        noise = np.random.default_rng([zlib.crc32(name.encode()), seed]).standard_normal(out[name].shape)
        drawn = base * np.exp(spread * noise) if base else spread * noise
        out[name] = jnp.asarray(drawn.astype(out[name].dtype))
    for name, factor in factors.items():
        out[name] = (out[name] * factor).astype(out[name].dtype)
    return out
```

```python
from contextlib import ExitStack

import concourse.bass as bass
from concourse import mybir

F32 = mybir.dt.float32
BF16 = mybir.dt.bfloat16
I32 = mybir.dt.int32
U32 = mybir.dt.uint32
ALU = mybir.AluOpType
ACT = mybir.ActivationFunctionType
AX = mybir.AxisListType.X

P = 128
EPS = 1e-5
NORM_MIN = 64.0
DENOM_MIN = 1e-6


def decoder_layer(nc, x, ctx_in, wq, wk, wv, wo, Wq, Wk, Wv, Wo, bo, Wr, br, W1, b1, W2, b2, out):
    B, N, C = x.shape
    H = 16
    D = C // H
    S = 32
    NK, CE = ctx_in.shape[1:]
    CEH = CE // 2
    INNER = Wq.shape[1]
    E, _, FF = W1.shape
    T = N // P
    CT = C // P
    G = H // 4
    QW = 512
    QH = N // QW
    QUADS = G * QH * T
    HP = H // 2
    FT = FF // P
    NKEY = H * NK
    PT = -(-NKEY // P)
    LAST = NKEY - (PT - 1) * P

    ctx = ExitStack()
    with ctx:
        def sb(name, shape, dt=F32):
            return ctx.enter_context(nc.sbuf_tensor(name, shape, dt))

        ident = sb("ident", [P, P])
        ident16 = sb("ident16", [P, P], BF16)
        wqkvT = sb("wqkvT", [P, CT, 3 * C])
        woT = sb("woT", [P, G, C])
        Wr_sb = sb("Wr_sb", [P, CT, E])
        br_sb = sb("br_sb", [1, E])
        bo_sb = sb("bo_sb", [P, C])
        neg_block = sb("neg_block", [P, P])
        den_pick = sb("den_pick", [P, P])
        x_raw = sb("x_raw", [P, T, C])
        x_res = sb("x_res", [P, T, C])
        x_hat = sb("x_hat", [P, T, C])
        xT = sb("xT", [P, CT, N])
        arena_a = sb("arena_a", [P, T * 2 * H * S])
        feat = arena_a[:, :].rearrange("p (w g t j s) -> p w g t j s", w=2, g=G, t=T, j=4)
        m_w = CT * NKEY
        Mb = arena_a[:, 0:m_w].rearrange("p (c k) -> p c k", c=CT)
        Nb = arena_a[:, m_w:m_w + PT * C].rearrange("p (i o) -> p i o", i=PT)
        pT = arena_a[:, m_w + PT * C:m_w + PT * C + 2 * PT * P].rearrange("p (b i q) -> p b i q", b=2, i=PT)
        v_aug = sb("v_aug", [P, T, H, S])
        NF, NS = D + 2, 6
        KR = NS * NF
        arena_b = sb("arena_b", [P, 2 * G * N])
        arena_s = sb("arena_s", [P, 7680])
        qT = arena_b[:, 0:G * N].rearrange("p (g n) -> p g n", g=G)
        opT = (arena_b[:, G * N:2 * G * N].bitcast(BF16).rearrange("p (w j n) -> p w j n", w=2, j=4),
               arena_s[:, 0:G * N].bitcast(BF16).rearrange("p (w j n) -> p w j n", w=2, j=4))
        n_parts = 2 * T * 4 * KR // 2
        parts = arena_s[:, G * N:G * N + n_parts].bitcast(BF16).rearrange(
            "p (w x s f) -> p w x s f", w=2, x=T * 4, s=NS)
        rest = sb("rest", [P, 2, T * 4, NF])
        hT = arena_b[:, :].rearrange("p (f n) -> p f n", f=FT)
        oT = sb("oT", [P, G, N])
        NBUF = 3
        arena_t = sb("arena_t", [P, NBUF * 4 * QW])
        root = arena_t[:, :].rearrange("p (b j q) -> p b (j q)", b=NBUF, j=4)
        sq = arena_t[:, 0:2 * 2 * C].rearrange("p (b c) -> p b c", b=2)
        Wq_nat = arena_a[:, 0:CT * INNER].rearrange("p (c i) -> p c i", c=CT)
        Wk_sb = arena_a[0:CEH, 2048:4096].rearrange("p (c i) -> p c i", c=2)
        Wv_sb = arena_a[0:CEH, 4096:6144].rearrange("p (c i) -> p c i", c=2)
        Wo_sb = arena_a[:, 6144:8192].rearrange("p (h o) -> p h o", h=HP)
        w_nat = arena_b[:, 0:3 * CT * C].rearrange("p (w c i) -> p w c i", w=3, c=CT)
        wo_pad = arena_b[:, 2048:2048 + CT * G * P].rearrange("p (c g j s) -> p c g j s", c=CT, g=G, j=4)
        WqT = arena_b[:, 4096:4096 + HP * C].rearrange("p (h c) -> p h c", h=HP)
        ctxT = arena_b[0:CEH, 6144:6144 + 2 * B * NK].rearrange("p (c b k) -> p c b k", c=2, b=B)
        ctx_sb = arena_b[0:NK, 3072:3072 + B * CE].rearrange("p (b c) -> p b c", b=B)
        kx = arena_t[:, 0:HP * B * NK].rearrange("p (h b k) -> p h b k", h=HP, b=B)
        vx = arena_t[:, HP * B * NK:2 * HP * B * NK].rearrange("p (h b k) -> p h b k", h=HP, b=B)
        prob = arena_t[:, 0:3 * NKEY].rearrange("p (b k) -> p b k", b=3)
        W1_sb = arena_t[:, 0:CT * FF].rearrange("p (c f) -> p c f", c=CT)
        W2_sb = arena_t[:, CT * FF:CT * FF + FT * C].rearrange("p (f o) -> p f o", f=FT)
        Gm = sb("Gm", [P, G, P])
        norms = sb("norms", [P, 2, G, T, 4])
        one_minus = sb("one_minus", [P, 2, G, T, 4])
        inv = sb("inv", [P, 2, G, T, 4])
        recip_den = x_hat[:, 0:QW // C, :].rearrange("p t c -> p (t c)")
        stats = sb("stats", [P, T, 6])
        meanvar = sb("meanvar", [P, T, 2])
        std = sb("std", [P, T])
        rstd = sb("rstd", [P, T])
        norm_low = sb("norm_low", [P, 1])
        low1 = sb("low1", [1, 1])
        fast_flag = sb("fast_flag", [1, 1], I32)
        pmax = sb("pmax", [P, 2, H])
        psumr = sb("psumr", [P, 2, H])
        pinv = sb("pinv", [P, 2, H])
        xsum = sb("xsum", [P, CT])
        route_s = sb("route_s", [1, E])
        route_m = sb("route_m", [1, 8])
        route_i = sb("route_i", [1, 8], U32)
        b1_rows = sb("b1_rows", [FT, P])
        b1_sb = sb("b1_sb", [P, FT])
        b2_sb = sb("b2_sb", [P, C])
        n_dram = nc.dram_tensor("n_rows_dram", (B, NKEY, C), F32, kind="Internal").ap()
        m_dram = nc.dram_tensor("m_cols_dram", (B, C, NKEY), F32, kind="Internal").ap()
        n_stage = [oT[0:NK, :, :].rearrange("p g n -> p (g n)").rearrange("p (h o) -> p h o", h=H),
                   arena_s[0:NK, 0:H * C].rearrange("p (h o) -> p h o", h=H)]
        m_stage = arena_s[:, 0:B * NKEY].rearrange("p (b h k) -> p b h k", b=B, h=H)
        SETS = (("n", 0, 0), ("m", 0, 1), ("n", 1, 0), ("m", 1, 1), ("n", 2, 0), ("n", 3, 1))

        def stored_before(n, st):
            return sum(which == st for _, _, which in SETS[:n])

        PS = ctx.enter_context(nc.psum_tensor("PS", [P, 8, 512], F32))

        PER = dict(
            x_in=16, presets=4,
            stats=3, std=3, xhat=3 * T, tr=3 * T, xt=3 * T,
            qk=T, v=T, squares=T, qk_out=T, norm=T, v_out=T,
            nlow=1, nlowT=1, flag=1, scaled=2,
            trq=2 * G, q_ready=2 * G, gmat=G, g_ready=G, split=G * 4, tr6=8 * G, op_ready=8 * G,
            sc_act=QUADS, sc_dve=QUADS, squared=QUADS, z_out=QUADS, z_sq=QUADS, rooted=QUADS, pv=QUADS,
            acc_out=G * QH, den=G * QH, rden=2 * G * QH, o_ready=G * QH,
            oproj=T, o_res=T,
            mn_in=48, bo_added=1,
            xsc=T, xmax=T, shifted=T, xexp=T, xsum=T, xinv=T, xnorm=T, ptr=3 * T, pt_out=3 * T, xo=T, x_res=T,
            xs=1, rsc=1, route=1, w_in=64, b1_tr=1, b1_out=1, b2_added=1,
            h_prod=2 * FT, h_out=2 * FT, y=T, y_res=T, stored=32,
            dve_step=1, batch_done=4,
        )
        sem = {k: ctx.enter_context(nc.semaphore("s_" + k)) for k in PER}
        once = {k: ctx.enter_context(nc.semaphore("s_" + k)) for k in
                ("weights", "setup", "wtr", "wtr_out", "kvx", "kvx_out", "mn", "m_out", "n_out", "stored0", "stored1")}
        SETUP_STEPS = 13
        PER["dve_step"] = 3 * (T + 2) + 3 + 6 + 3 + 5 * G
        go, gone = (ctx.enter_context(nc.semaphore("s_" + k)) for k in ("go", "gone"))
        first, last_sem = sem["x_in"].num, sem["batch_done"].num
        assert last_sem - first == len(sem) - 1

        def after(eng, name, n):
            assert 0 < n <= PER[name]
            eng.wait_ge(sem[name], n)

        def batch_end(eng):
            eng.drain().then_inc(sem["batch_done"], 1)
            eng.wait_ge(go, 1)
            eng.sem_inc(gone, 1)

        N_WEIGHT_DMAS = 3 + CT * G + 1 + 2 + 1 + 3 + 1

        block = ctx.enter_context(nc.Block())

        @block.sync
        def _(sp):
            for i, w in enumerate((wq, wk, wv)):
                sp.dma_start(w_nat[:, i], w.rearrange("(c p) i -> p c i", p=P)).then_inc(once["weights"], 16)
            sp.wait_ge(once["setup"], 1)
            for c in range(CT):
                for g in range(G):
                    sp.dma_start(wo_pad[:, c, g, :, 0:D], wo[c * P:(c + 1) * P, g * 4 * D:(g + 1) * 4 * D]
                                 .rearrange("p (j d) -> p j d", j=4)).then_inc(once["weights"], 16)
            sp.dma_start(Wq_nat, Wq.rearrange("(c p) i -> p c i", p=P)).then_inc(once["weights"], 16)
            for dst, w in ((Wk_sb, Wk), (Wv_sb, Wv)):
                sp.dma_start(dst, w.rearrange("(c p) i -> p c i", p=CEH)).then_inc(once["weights"], 16)
            sp.dma_start(Wo_sb, Wo.rearrange("(h p) o -> p h o", p=P)).then_inc(once["weights"], 16)
            sp.dma_start(Wr_sb[:, :, :], Wr.rearrange("(c p) e -> p c e", p=P)).then_inc(once["weights"], 16)
            sp.dma_start(br_sb[:, :], br.rearrange("(a e) -> a e", a=1)).then_inc(once["weights"], 16)
            sp.dma_start(bo_sb[:, :], bo.rearrange("(a c) -> a c", a=1).to_broadcast([P, C])).then_inc(once["weights"], 16)
            sp.dma_start(ctx_sb, ctx_in.rearrange("b k c -> k b c")).then_inc(once["weights"], 16)
            done_n, done_m = 0, 0
            for kind, i, st in SETS:
                if kind == "n":
                    done_n += H // 2
                    sp.wait_ge(once["n_out"], done_n)
                    sp.dma_start(n_dram[i].rearrange("(h k) o -> k h o", h=H), n_stage[st]).then_inc(once[f"stored{st}"], 16)
                else:
                    done_m += H
                    sp.wait_ge(once["m_out"], done_m)
                    sp.dma_start(m_dram[:, i * P:(i + 1) * P, :].rearrange("b p k -> p b k"),
                                 m_stage.rearrange("p b h k -> p b (h k)")).then_inc(once["stored1"], 16)
            for st in range(2):
                sp.wait_ge(once[f"stored{st}"], 16 * stored_before(len(SETS), st))
            with sp.Fori(0, B) as b:
                sp.dma_start(x_raw[:, :, :], x[bass.ds(b, 1)].rearrange("a (t p) c -> p (a t) c", p=P)
                             ).then_inc(sem["x_in"], 16)
                after(sp, "split", 4 * G)
                after(sp, "gmat", G)
                sp.dma_start(Mb, m_dram[bass.ds(b, 1)].rearrange("a (c p) k -> p (a c) k", p=P)).then_inc(sem["mn_in"], 16)
                sp.dma_start(Nb[:, 0:PT - 1, :], n_dram[bass.ds(b, 1), 0:(PT - 1) * P, :]
                             .rearrange("a (i p) o -> p (a i) o", p=P)).then_inc(sem["mn_in"], 16)
                sp.dma_start(Nb[0:LAST, PT - 1, :], n_dram[bass.ds(b, 1), (PT - 1) * P:NKEY, :]
                             .rearrange("a p o -> (a p) o")).then_inc(sem["mn_in"], 16)
                after(sp, "route", 1)
                e = sp.value_load(route_i[0:1, 0:1], min_val=0, max_val=E - 1)
                sp.dma_start(W1_sb, W1[bass.ds(e, 1)].rearrange("a (c p) f -> p (a c) f", p=P)).then_inc(sem["w_in"], 16)
                sp.dma_start(b1_rows[:, :], b1[bass.ds(e, 1)].rearrange("a (f p) -> (a f) p", p=P)).then_inc(sem["w_in"], 16)
                sp.dma_start(b2_sb[:, :], b2[bass.ds(e, 1)].to_broadcast([P, C])).then_inc(sem["w_in"], 16)
                sp.dma_start(W2_sb, W2[bass.ds(e, 1)].rearrange("a (f p) o -> p (a f) o", p=P)).then_inc(sem["w_in"], 16)
                for half in range(2):
                    t0 = half * T // 2
                    after(sp, "y_res", t0 + T // 2)
                    sp.dma_start(out[bass.ds(b, 1)].rearrange("a (t p) c -> p (a t) c", p=P)[:, t0:t0 + T // 2],
                                 x_res[:, t0:t0 + T // 2, :]).then_inc(sem["stored"], 16)
                after(sp, "stored", PER["stored"])
                after(sp, "batch_done", 4)
                sp.sem_clear(range(first, last_sem + 1))
                sp.sem_inc(go, 1)
                sp.wait_ge(gone, 4)
                sp.sem_clear(go)
                sp.sem_clear(gone)

        @block.gpsimd
        def _(pool):
            done = [0]

            def setup(ins):
                done[0] += 1
                ins.then_inc(once["setup"], 1)
                pool.wait_ge(once["setup"], done[0])

            setup(pool.memset(wo_pad, 0.0))
            setup(pool.memset(ident[:, :], 0.0))
            setup(pool.affine_select(out=ident[:, :], in_=ident[:, :], compare_op=ALU.not_equal, fill=1.0,
                                     base=0, pattern=[[-1, P]], channel_multiplier=1))
            setup(pool.tensor_copy(ident16[:, :], ident[:, :]))
            setup(pool.memset(den_pick[:, :], 0.0))
            pick = den_pick[:, :].rearrange("p (j m) -> p j m", j=4)
            setup(pool.affine_select(out=pick, in_=pick, compare_op=ALU.not_equal, fill=1.0, base=-D,
                                     pattern=[[-S, 4], [0, S]], channel_multiplier=1))
            setup(pool.memset(neg_block[:, :], 0.0))
            for j in range(4):
                setup(pool.memset(neg_block[j * S:(j + 1) * S, j * S:(j + 1) * S], -1.0))
            setup(pool.memset(v_aug[:, :, :, D:S].rearrange("p t h s -> p (t h) s"), 0.0))
            setup(pool.memset(v_aug[:, :, :, D:D + 1].rearrange("p t h s -> p (t h) s"), 1.0))
            assert done[0] == SETUP_STEPS
            pool.wait_ge(once["m_out"], 2 * H)
            pool.wait_ge(once["n_out"], B * H // 2)
            with pool.Fori(0, B) as b:
                flat = feat.rearrange("p w g t j s -> p (w g t j) s")
                half = flat.shape[1] // 2
                presets = ((flat[:, :, D + 3:S], 0.0), (flat[:, :, D + 2:D + 3], 1.0),
                           (flat[:, 0:half, D + 1:D + 2], 1.0), (flat[:, half:2 * half, D:D + 1], 2.0))
                for i, (places, value) in enumerate(presets):
                    pool.memset(places, value).then_inc(sem["presets"], 1)
                    after(pool, "presets", i + 1)
                for q in range(QUADS):
                    after(pool, "z_out", q + 1)
                    zt = root[:, q % NBUF, 2 * QW:4 * QW]
                    pool.tensor_tensor(zt, zt, zt, ALU.mult).then_inc(sem["z_sq"], 1)
                after(pool, "xhat", 2 * T)
                pool.tensor_tensor(x_res[:, :, :], x_res[:, :, :],
                                   bo_sb[:, None, :].to_broadcast([P, T, C]), ALU.add).then_inc(sem["bo_added"], 1)
                after(pool, "xhat", 3 * T)
                after(pool, "w_in", PER["w_in"])
                pool.tensor_tensor(x_res[:, :, :], x_res[:, :, :],
                                   b2_sb[:, None, :].to_broadcast([P, T, C]), ALU.add).then_inc(sem["b2_added"], 1)
                batch_end(pool)

        @block.scalar
        def _(act):
            for i in range(3):
                act.wait_ge(once["wtr"], i + 1)
                act.activation(wqkvT[:, :, i * C:(i + 1) * C], PS[:, i, :].rearrange("p (c o) -> p c o", c=CT),
                               ACT.Copy).then_inc(once["wtr_out"], 1)
            for i in range(2):
                act.wait_ge(once["wtr"], 4 + i)
                act.activation(woT[:, 2 * i:2 * i + 2, :], PS[:, 3 + i, :].rearrange("p (g o) -> p g o", g=2),
                               ACT.Copy).then_inc(once["wtr_out"], 1)
            for i in range(4):
                act.wait_ge(once["wtr"], 6 + i)
                act.activation(WqT[:, 2 * i:2 * i + 2, :], PS[:, (5 + i) % 8, :].rearrange("p (g o) -> p g o", g=2),
                               ACT.Copy).then_inc(once["wtr_out"], 1)
            for c in range(2):
                act.wait_ge(once["wtr"], 10 + c)
                act.activation(ctxT[:, c], PS[0:CEH, 1 + c, 0:B * NK].rearrange("p (b k) -> p b k", b=B), ACT.Copy
                               ).then_inc(once["wtr_out"], 1)
            for i in range(2 * HP):
                act.wait_ge(once["kvx"], i + 1)
                act.activation((kx, vx)[i // HP][:, i % HP], PS[:, i % 4, 0:B * NK].rearrange("p (b k) -> p b k", b=B),
                               ACT.Copy).then_inc(once["kvx_out"], 1)
            at, stored = 0, 0
            for n, (kind, i, st) in enumerate(SETS):
                if kind == "m":
                    at += H
                    continue
                if stored_before(n, st):
                    act.wait_ge(once[f"stored{st}"], 16 * stored_before(n, st))
                for k in range(H // 2):
                    at += 1
                    act.wait_ge(once["mn"], at)
                    heads = 4 * (k // 2) + k % 2
                    act.activation(n_stage[st][:, heads:heads + 3:2, :],
                                   PS[0:NK, 4 + k % 4, :].rearrange("p (h o) -> p h o", h=2), ACT.Copy
                                   ).then_inc(once["n_out"], 1)

            with act.Fori(0, B) as b:
                def layer_norm_std(i):
                    after(act, "stats", i + 1)
                    act.activation(std[:, :], meanvar[:, :, 1], ACT.Sqrt, bias=EPS).then_inc(sem["std"], 1)

                def xT_out(i, t):
                    after(act, "tr", i * T + t + 1)
                    act.activation(xT[:, :, t * P:(t + 1) * P], PS[:, t % 2, 0:C].rearrange("p (c n) -> p c n", c=CT),
                                   ACT.Copy).then_inc(sem["xt"], 1)

                layer_norm_std(0)
                xT_out(0, 0)
                for t in range(T):
                    if t + 1 < T:
                        xT_out(0, t + 1)
                    after(act, "qk", t + 1)
                    if t >= 2:
                        after(act, "norm", t - 1)
                    src = PS[:, 2 + t % 2, :]
                    act.activation(sq[:, t % 2, :], src, ACT.Square).then_inc(sem["squares"], 1)
                    if t == 0:
                        after(act, "presets", 4)
                    act.activation(feat[:, 0, :, t, :, 0:D], src[:, 0:C].rearrange("p (g j d) -> p g j d", g=G, j=4), ACT.Copy)
                    act.activation(feat[:, 1, :, t, :, 0:D], src[:, C:2 * C].rearrange("p (g j d) -> p g j d", g=G, j=4),
                                   ACT.Copy, scale=-4.0).then_inc(sem["qk_out"], 1)
                for f in range(2 * G):
                    half, g = f // G, f % G
                    after(act, "trq", f + 1)
                    act.activation(qT[:, g, half * 512:(half + 1) * 512], PS[:, f % 2, :], ACT.Copy
                                   ).then_inc(sem["q_ready"], 1)

                def square(q):
                    after(act, "sc_act", q + 1)
                    if q >= NBUF:
                        after(act, "pv", q - NBUF + 1)
                    act.activation(root[:, q % NBUF, 0:2 * QW],
                                   PS[:, 2 * (q % 2):2 * (q % 2) + 2, :].rearrange("p j q -> p (j q)"),
                                   ACT.Square, bias=1.0).then_inc(sem["squared"], 1)

                def take_root(q):
                    after(act, "squared", q + 1)
                    after(act, "z_sq", q + 1)
                    act.activation(root[:, q % NBUF, :], root[:, q % NBUF, :], ACT.Sqrt, bias=-1.0
                                   ).then_inc(sem["rooted"], 1)

                for q in range(QUADS):
                    square(q)
                    if q >= 1:
                        take_root(q - 1)
                take_root(QUADS - 1)

                layer_norm_std(1)
                for t in range(T):
                    xT_out(1, t)

                def p_out(t, i):
                    n = min(4, PT - 4 * i)
                    after(act, "ptr", 3 * t + i + 1)
                    act.activation(pT[:, t % 2, 4 * i:4 * i + n, :],
                                   PS[:, 4 + (3 * t + i) % 2, 0:n * P].rearrange("p (i q) -> p i q", i=n), ACT.Copy
                                   ).then_inc(sem["pt_out"], 1)

                for t in range(T + 1):
                    if t < T:
                        after(act, "shifted", t + 1)
                        act.activation(prob[:, t % 3, :], prob[:, t % 3, :], ACT.Exp).then_inc(sem["xexp"], 1)
                    if t >= 1:
                        if t >= 3:
                            after(act, "xo", t - 2)
                        for i in range(3):
                            p_out(t - 1, i)
                layer_norm_std(2)
                for t in range(T):
                    xT_out(2, t)
                after(act, "b1_tr", 1)
                act.activation(b1_sb[:, :], PS[:, 6, 0:FT], ACT.Copy).then_inc(sem["b1_out"], 1)
                after(act, "b1_out", 1)
                for f in range(0, 2 * FT, 2):
                    after(act, "h_prod", f + 1)
                    act.activation(hT[:, f // 2, 0:512], PS[:, f % 4, :], ACT.Relu,
                                   bias=b1_sb[:, f // 2:f // 2 + 1]).then_inc(sem["h_out"], 1)
                    after(act, "h_prod", f + 2)
                    act.activation(hT[:, f // 2, 512:1024], PS[:, (f + 1) % 4, :], ACT.Relu,
                                   bias=b1_sb[:, f // 2:f // 2 + 1]).then_inc(sem["h_out"], 1)
                batch_end(act)


        @block.vector
        def _(dve):
            at = 0
            for n, (kind, i, st) in enumerate(SETS):
                if kind == "n":
                    at += H // 2
                    continue
                if stored_before(n, st):
                    dve.wait_ge(once[f"stored{st}"], 16 * stored_before(n, st))
                for k in range(H):
                    at += 1
                    dve.wait_ge(once["mn"], at)
                    dve.tensor_scalar(m_stage[:, :, k, :], PS[:, k % 4, 0:B * NK].rearrange("p (b k) -> p b k", b=B),
                                      float(INNER // H) ** -0.5, None, ALU.mult).then_inc(once["m_out"], 1)
            with dve.Fori(0, B) as b:
                steps = [0]

                def step(ins):
                    steps[0] += 1
                    ins.then_inc(sem["dve_step"], 1)
                    after(dve, "dve_step", steps[0])

                def tile_stats(src, t):
                    return dve.bn_stats(stats[:, t, :], src[:, t, :])

                def layer_norm(i, src):
                    for t in range(T):
                        step(dve.bn_aggr(meanvar[:, t, :], stats[:, t, :])) if t == 0 else \
                            dve.bn_aggr(meanvar[:, t, :], stats[:, t, :]).then_inc(
                                sem["stats" if t == T - 1 else "dve_step"], 1)
                        if 0 < t < T - 1:
                            steps[0] += 1
                    after(dve, "std", i + 1)
                    step(dve.reciprocal(rstd[:, :], std[:, :]))
                    if i:
                        after(dve, "tr", i * T)
                    for t in range(T):
                        dve.tensor_scalar(x_hat[:, t, :], src[:, t, :], meanvar[:, t, 0:1], rstd[:, t:t + 1],
                                          ALU.subtract, ALU.mult).then_inc(sem["xhat"], 1)

                dve.wait_ge(once["setup"], SETUP_STEPS)
                after(dve, "x_in", 16)
                for t in range(T - 1):
                    tile_stats(x_raw, t)
                step(tile_stats(x_raw, T - 1))
                layer_norm(0, x_raw)
                for t in range(T):
                    after(dve, "squares", t + 1)
                    dve.tensor_reduce(norms[:, :, :, t, :].rearrange("p w g j -> p (w g) j"),
                                      sq[:, t % 2, :].rearrange("p (h j d) -> p h j d", j=4, d=D), AX, ALU.add
                                      ).then_inc(sem["norm"], 1)
                    after(dve, "v", t + 1)
                    dve.tensor_copy(v_aug[:, t, :, 0:D], PS[:, 4 + t % 2, 0:C].rearrange("p (h d) -> p h d", h=H)
                                    ).then_inc(sem["v_out"], 1)
                after(dve, "norm", T)
                norms_flat, om_flat, inv_flat = (a[:, :, :, :, :].rearrange("p w g t j -> p (w g t j)")
                                                 for a in (norms, one_minus, inv))
                half_n = T * H
                flat = feat.rearrange("p w g t j s -> p (w g t j) s")
                dve.tensor_reduce(norm_low[:, :], norms_flat, AX, ALU.min
                                  ).then_inc(sem["nlow"], 1)
                step(dve.tensor_scalar(om_flat, norms_flat, -1.0, 1.0, ALU.mult, ALU.add))
                step(dve.reciprocal(inv_flat, om_flat))
                after(dve, "presets", 4)
                dve.tensor_copy(flat[:, 0:half_n, D], norms_flat[:, 0:half_n])
                step(dve.tensor_scalar(flat[:, half_n:2 * half_n, D + 1], norms_flat[:, half_n:2 * half_n], 2.0, None, ALU.mult))
                after(dve, "nlowT", 1)
                step(dve.tensor_reduce(low1[:, :], PS[0:1, 6, 0:P], AX, ALU.min))
                dve.tensor_scalar(fast_flag[:, :], low1[:, :], NORM_MIN, None, ALU.is_ge).then_inc(sem["flag"], 1)
                after(dve, "qk_out", T)
                for w in range(2):
                    part = flat[:, w * half_n:(w + 1) * half_n, 0:NF]
                    dve.tensor_tensor(part, part, inv_flat[:, w * half_n:(w + 1) * half_n, None]
                                      .to_broadcast([P, half_n, NF]), ALU.mult).then_inc(sem["scaled"], 1)
                after(dve, "scaled", 2)

                def group(g):
                    return feat[:, :, g, :, :, 0:NF].rearrange("p w t j s -> p w (t j) s")

                def high_q(g):
                    f = group(g)[:, 0]
                    dve.tensor_copy(parts[:, 0, :, 0:4:3, :], f[:, :, None, :].to_broadcast([P, T * 4, 2, NF])
                                    ).then_inc(sem["dve_step"], 1)
                    dve.tensor_copy(parts[:, 0, :, 5, :], f).then_inc(sem["dve_step"], 1)
                    steps[0] += 2

                def high_k(g):
                    f = group(g)[:, 1]
                    step(dve.tensor_copy(parts[:, 1, :, 0:3, :], f[:, :, None, :].to_broadcast([P, T * 4, 3, NF])))

                def less_high(g):
                    step(dve.tensor_tensor(rest[:, :, :, :], group(g), parts[:, :, :, 0, :], ALU.subtract))

                def middle(g):
                    dve.tensor_copy(parts[:, 0, :, 1:5:3, :], rest[:, 0, :, None, :].to_broadcast([P, T * 4, 2, NF])
                                    ).then_inc(sem["split"], 1)
                    dve.tensor_copy(parts[:, 1, :, 3:5, :], rest[:, 1, :, None, :].to_broadcast([P, T * 4, 2, NF])
                                    ).then_inc(sem["split"], 1)
                    after(dve, "split", 4 * g + 2)

                def low(g):
                    for w, m, l in ((0, 1, 2), (1, 3, 5)):
                        dve.tensor_tensor(parts[:, w, :, l, :], rest[:, w], parts[:, w, :, m, :], ALU.subtract
                                          ).then_inc(sem["split"], 1)

                def operand_out(g, e):
                    after(dve, "tr6", 8 * g + e + 1)
                    dve.tensor_copy(opT[g % 2][0:KR, e // 4, e % 4, :], PS[0:KR, 7, :].bitcast(BF16)
                                    ).then_inc(sem["op_ready"], 1)

                high_q(0)
                high_k(0)
                less_high(0)
                middle(0)
                low(0)
                for g in range(G):
                    after(dve, "gmat", g + 1)
                    dve.tensor_tensor(Gm[:, g, :], PS[:, 4 + g % 2, 0:P], neg_block[:, :], ALU.mult
                                      ).then_inc(sem["g_ready"], 1)

                for e in range(8):
                    operand_out(0, e)

                def acc_out(i):
                    g, qh = i // QH, i % QH
                    after(dve, "pv", T * (i + 1))
                    dve.tensor_copy(oT[:, g, qh * QW:(qh + 1) * QW], PS[:, 6, :]).then_inc(sem["acc_out"], 1)

                def recip(i, part):
                    if part == 0:
                        after(dve, "den", i + 1)
                        if i:
                            after(dve, "o_ready", i)
                    cols = slice(part * QW // 2, (part + 1) * QW // 2)
                    dve.reciprocal(recip_den[:, cols], PS[:, 7, cols]).then_inc(sem["rden"], 1)

                def normalise(i):
                    g, qh = i // QH, i % QH
                    after(dve, "rden", 2 * i + 2)
                    part = oT[:, g, qh * QW:(qh + 1) * QW]
                    dve.tensor_tensor(part, part, recip_den, ALU.mult).then_inc(sem["o_ready"], 1)

                for q in range(QUADS):
                    after(dve, "sc_dve", q + 1)
                    if q >= NBUF:
                        after(dve, "pv", q - NBUF + 1)
                    dve.tensor_scalar(root[:, q % NBUF, 2 * QW:4 * QW],
                                      PS[:, 4:6, :].rearrange("p j q -> p (j q)"), 0.0, 1.0, ALU.max, ALU.add
                                      ).then_inc(sem["z_out"], 1)
                    at, g = q % (QH * T), q // (QH * T)
                    prev = g * QH - 2
                    if q >= T and q % T == 1:
                        acc_out(q // T - 1)
                    if g:
                        if at in (0, 1):
                            recip(prev, at)
                        if at in (3, 4):
                            recip(prev + 1, at - 3)
                        if at in (2, 5):
                            normalise(prev + (at == 5))
                    if g + 1 < G:
                        for when, make in ((2, high_q), (5, high_k), (6, less_high), (7, middle), (7, low)):
                            if at == when:
                                make(g + 1)
                        if at >= 8:
                            operand_out(g + 1, at - 8)
                for i in (G * QH - 2, G * QH - 1):
                    if i % 2:
                        acc_out(i)
                    recip(i, 0)
                    recip(i, 1)
                    normalise(i)

                for t in range(T):
                    after(dve, "oproj", t + 1)
                    dve.tensor_tensor(x_res[:, t, :], PS[:, 4 + t % 2, 0:C], x_raw[:, t, :], ALU.add
                                      ).then_inc(sem["o_res"], 1)
                    if t >= 1:
                        after(dve, "o_res", t)
                        tile_stats(x_res, t - 1)
                after(dve, "o_res", T)
                step(tile_stats(x_res, T - 1))
                layer_norm(1, x_res)
                def sc(t):
                    return PS[:, 0:4, 0:4 * NK].rearrange("p c (h k) -> p c h k", h=4)

                def x_sum(t):
                    after(dve, "xexp", t + 1)
                    pr = prob[:, t % 3, :].rearrange("p (h k) -> p h k", h=H)
                    dve.tensor_reduce(psumr[:, t % 2, :], pr, AX, ALU.add).then_inc(sem["xsum"], 1)
                    after(dve, "xsum", t + 1)
                    dve.reciprocal(pinv[:, t % 2, :], psumr[:, t % 2, :]).then_inc(sem["xinv"], 1)
                    after(dve, "xinv", t + 1)
                    dve.tensor_tensor(pr, pr, pinv[:, t % 2, :, None].to_broadcast([P, H, NK]), ALU.mult
                                      ).then_inc(sem["xnorm"], 1)

                def x_residual(t):
                    after(dve, "xo", t + 1)
                    if t == 0:
                        after(dve, "bo_added", 1)
                    dve.tensor_tensor(x_res[:, t, :], PS[:, 6 + t % 2, 0:C], x_res[:, t, :], ALU.add
                                      ).then_inc(sem["x_res"], 1)
                    after(dve, "x_res", t + 1)
                    return tile_stats(x_res, t)

                for t in range(T):
                    after(dve, "xsc", t + 1)
                    dve.tensor_reduce(pmax[:, t % 2, :].rearrange("p (c h) -> p c h", c=4), sc(t), AX, ALU.max
                                      ).then_inc(sem["xmax"], 1)
                    after(dve, "xmax", t + 1)
                    if t >= 3:
                        after(dve, "ptr", 3 * (t - 2))
                    dve.tensor_tensor(prob[:, t % 3, :].rearrange("p (c h k) -> p c h k", c=4, h=4), sc(t),
                                      pmax[:, t % 2, :].rearrange("p (c h) -> p c h", c=4)[:, :, :, None]
                                      .to_broadcast([P, 4, 4, NK]), ALU.subtract).then_inc(sem["shifted"], 1)
                    if t >= 2:
                        x_residual(t - 2)
                    x_sum(t)
                x_residual(T - 2)
                step(x_residual(T - 1))
                layer_norm(2, x_res)
                after(dve, "xt", 3 * T)
                dve.tensor_reduce(xsum[:, :], xT[:, :, :], AX, ALU.add).then_inc(sem["xs"], 1)
                after(dve, "rsc", 1)
                step(dve.scalar_tensor_tensor(route_s[:, :], PS[0:1, 7, 0:E], 1.0 / N, br_sb[:, :], ALU.mult, ALU.add))
                step(dve.max(route_m[:, :], route_s[:, :]))
                dve.max_index(route_i[:, :], route_m[:, :], route_s[:, :]).then_inc(sem["route"], 1)
                after(dve, "b2_added", 1)
                for t in range(T):
                    after(dve, "y", t + 1)
                    dve.tensor_tensor(x_res[:, t, :], PS[:, 4 + t % 2, 0:C], x_res[:, t, :], ALU.add
                                      ).then_inc(sem["y_res"], 1)
                batch_end(dve)

        @block.tensor
        def _(pe):
            pe.wait_ge(once["setup"], SETUP_STEPS)
            pe.wait_ge(once["weights"], 16 * N_WEIGHT_DMAS)
            for i in range(3):
                for c in range(CT):
                    for o in range(CT):
                        last = pe.transpose(PS[:, i, c * C + o * P:c * C + (o + 1) * P],
                                            w_nat[:, i, o, c * P:(c + 1) * P], ident[:, :])
                last.then_inc(once["wtr"], 1)
            for i in range(2):
                for g in (2 * i, 2 * i + 1):
                    for o in range(CT):
                        last = pe.transpose(PS[:, 3 + i, (g % 2) * C + o * P:(g % 2) * C + (o + 1) * P],
                                            wo_pad[:, o, g].rearrange("p j s -> p (j s)"), ident[:, :])
                last.then_inc(once["wtr"], 1)
            for i in range(4):
                if i == 3:
                    pe.wait_ge(once["wtr_out"], 1)
                for h in (2 * i, 2 * i + 1):
                    for c in range(CT):
                        last = pe.transpose(PS[:, (5 + i) % 8, (h % 2) * C + c * P:(h % 2) * C + (c + 1) * P],
                                            Wq_nat[:, c, h * P:(h + 1) * P], ident[:, :])
                last.then_inc(once["wtr"], 1)
            pe.wait_ge(once["wtr_out"], 3)
            for c in range(2):
                for b in range(B):
                    last = pe.transpose(PS[0:CEH, 1 + c, b * NK:(b + 1) * NK], ctx_sb[:, b, c * CEH:(c + 1) * CEH],
                                        ident[0:NK, 0:NK])
                last.then_inc(once["wtr"], 1)
            pe.wait_ge(once["wtr_out"], 11)
            for i in range(2 * HP):
                if i >= 4:
                    pe.wait_ge(once["kvx_out"], i - 3)
                w, hp = (Wk_sb, Wv_sb)[i // HP], i % HP
                for c in range(2):
                    last = pe.matmul(PS[:, i % 4, 0:B * NK], w[:, c, hp * P:(hp + 1) * P],
                                     ctxT[:, c].rearrange("p b k -> p (b k)"), start=(c == 0), stop=(c == 1))
                last.then_inc(once["kvx"], 1)
            pe.wait_ge(once["kvx_out"], 2 * HP)
            n_done, m_done = 0, 0
            for kind, i, st in SETS:
                if kind == "n":
                    for k in range(H // 2):
                        if n_done >= 4:
                            pe.wait_ge(once["n_out"], n_done - 3)
                        odd = k % 2
                        for h in range(2):
                            hp = 2 * (k // 2) + h
                            last = pe.matmul(PS[0:NK, 4 + k % 4, h * C:(h + 1) * C],
                                             vx[64 * odd:64 * odd + 64, hp, i, :], Wo_sb[64 * odd:64 * odd + 64, hp, :],
                                             start=True, stop=True)
                        last.then_inc(once["mn"], 1)
                        n_done += 1
                else:
                    for h in range(H):
                        if m_done >= 4:
                            pe.wait_ge(once["m_out"], m_done - 3)
                        odd = h % 2
                        pe.matmul(PS[:, h % 4, 0:B * NK], WqT[64 * odd:64 * odd + 64, h // 2, i * P:(i + 1) * P],
                                  kx[64 * odd:64 * odd + 64, h // 2].rearrange("p b k -> p (b k)"),
                                  start=True, stop=True).then_inc(once["mn"], 1)
                        m_done += 1
            pe.wait_ge(once["m_out"], 2 * H)
            pe.wait_ge(once["n_out"], B * H // 2)

            with pe.Fori(0, B) as b:
                def transpose_x(i, t):
                    after(pe, "xhat", i * T + t + 1)
                    if i * T + t >= 2:
                        after(pe, "xt", i * T + t - 1)
                    for c in range(CT):
                        last = pe.transpose(PS[:, t % 2, c * P:(c + 1) * P], x_hat[:, t, c * P:(c + 1) * P], ident[:, :])
                    last.then_inc(sem["tr"], 1)

                transpose_x(0, 0)
                for t in range(T):
                    if t + 1 < T:
                        transpose_x(0, t + 1)
                    after(pe, "xt", t + 1)
                    if t >= 2:
                        after(pe, "qk_out", t - 1)
                    for c in range(CT):
                        last = pe.matmul(PS[:, 2 + t % 2, :], xT[:, c, t * P:(t + 1) * P], wqkvT[:, c, 0:2 * C],
                                         start=(c == 0), stop=(c == CT - 1))
                    last.then_inc(sem["qk"], 1)
                    if t >= 2:
                        after(pe, "v_out", t - 1)
                    for c in range(CT):
                        last = pe.matmul(PS[:, 4 + t % 2, 0:C], xT[:, c, t * P:(t + 1) * P], wqkvT[:, c, 2 * C:3 * C],
                                         start=(c == 0), stop=(c == CT - 1))
                    last.then_inc(sem["v"], 1)
                after(pe, "nlow", 1)
                pe.transpose(PS[0:1, 6, 0:P], norm_low[:, :], ident[:, :]).then_inc(sem["nlowT"], 1)
                after(pe, "xt", T)
                after(pe, "qk_out", T)
                for f in range(2 * G):
                    half, g = f // G, f % G
                    if f == 0:
                        after(pe, "scaled", 1)
                    if f >= 2:
                        after(pe, "q_ready", f - 1)
                    for i in range(T // 2):
                        last = pe.transpose(PS[:, f % 2, i * P:(i + 1) * P],
                                            feat[:, 0, g, half * T // 2 + i].rearrange("p j s -> p (j s)"), ident[:, :])
                    last.then_inc(sem["trq"], 1)
                after(pe, "v_out", T)
                after(pe, "scaled", 2)
                for g in range(G):
                    if g >= 2:
                        after(pe, "g_ready", g - 1)
                    for t in range(T):
                        last = pe.matmul(PS[:, 4 + g % 2, 0:P],
                                         feat[:, 1, g, t].rearrange("p j s -> p (j s)"),
                                         v_aug[:, t, 4 * g:4 * g + 4, :].rearrange("p h s -> p (h s)"),
                                         start=(t == 0), stop=(t == T - 1))
                    last.then_inc(sem["gmat"], 1)

                def turn_operand(g, e):
                    if e == 0:
                        after(pe, "split", 4 * g + 4)
                    if g or e:
                        after(pe, "op_ready", 8 * g + e)
                    if g > 1 and e == 0:
                        after(pe, "rden", 4 * (g - 1))
                    for t in range(T):
                        last = pe.transpose(PS[0:KR, 7, :].bitcast(BF16)[:, t * P:(t + 1) * P],
                                            parts[:, e // 4, 4 * t + e % 4].rearrange("p s f -> p (s f)"), ident16[:, :])
                    last.then_inc(sem["tr6"], 1)

                after(pe, "flag", 1)
                for e in range(8):
                    turn_operand(0, e)
                after(pe, "q_ready", 2 * G)
                after(pe, "g_ready", G)

                def scores(q):
                    g, qh, kt = q // (QH * T), q // T % QH, q % T
                    if q >= 2:
                        after(pe, "squared", q - 1)
                    if q % (QH * T) == 0:
                        after(pe, "op_ready", 8 * (g + 1))
                    for j in range(4):
                        if j == 2 and q >= 1:
                            after(pe, "z_out", q)
                        bank = 2 * (q % 2) + j if j < 2 else 2 + j
                        mm = pe.matmul(PS[:, bank, :], opT[g % 2][0:KR, 1, j, kt * P:(kt + 1) * P],
                                       opT[g % 2][0:KR, 0, j, qh * QW:(qh + 1) * QW], start=True, stop=True)
                        if j % 2:
                            mm.then_inc(sem["sc_act" if j == 1 else "sc_dve"], 1)

                def weigh(q):
                    g, qh, kt = q // (QH * T), q // T % QH, q % T
                    i = q // T
                    acc = PS[:, 6, :]
                    if kt == 0:
                        if i >= 1:
                            after(pe, "acc_out", i)
                        pe.matmul(acc, Gm[:, g, :], qT[:, g, qh * QW:(qh + 1) * QW], start=True, stop=False,
                                  skip_group_check=True)
                    after(pe, "rooted", q + 1)
                    for j in range(4):
                        mm = pe.matmul(acc[j * S:(j + 1) * S, :], v_aug[:, kt, 4 * g + j, :],
                                       root[:, q % NBUF, j * QW:(j + 1) * QW], start=False, stop=(kt == T - 1),
                                       skip_group_check=True)
                    mm.then_inc(sem["pv"], 1)

                def denominators(i):
                    g, qh = i // QH, i % QH
                    after(pe, "acc_out", i + 1)
                    if i:
                        after(pe, "rden", 2 * i)
                    after(pe, "op_ready", 8 * min(G, i // QH + 2))
                    pe.matmul(PS[:, 7, :], den_pick[:, :], oT[:, g, qh * QW:(qh + 1) * QW],
                              start=True, stop=True).then_inc(sem["den"], 1)

                for q in range(QUADS + 2):
                    if q < QUADS:
                        scores(q)
                    if q >= 2:
                        weigh(q - 2)
                    at, gq = q % (QH * T), q // (QH * T)
                    if 0 < gq < G and at in (0, 3):
                        denominators(gq * QH - 2 + (at == 3))
                    if gq + 1 < G and at >= 8:
                        turn_operand(gq + 1, at - 8)
                denominators(G * QH - 2)
                denominators(G * QH - 1)

                after(pe, "squared", QUADS)
                after(pe, "z_out", QUADS)
                after(pe, "o_ready", G * QH)
                for t in range(T):
                    if t >= 2:
                        after(pe, "o_res", t - 1)
                    for g in range(G):
                        last = pe.matmul(PS[:, 4 + t % 2, 0:C], oT[:, g, t * P:(t + 1) * P], woT[:, g, :],
                                         start=(g == 0), stop=(g == G - 1))
                    last.then_inc(sem["oproj"], 1)
                for t in range(T):
                    transpose_x(1, t)
                after(pe, "xt", 2 * T)

                def x_scores(t):
                    if t >= 1:
                        after(pe, "shifted", t)
                    for i in range(4):
                        for c in range(CT):
                            last = pe.matmul(PS[:, i, 0:4 * NK], xT[:, c, t * P:(t + 1) * P],
                                             Mb[:, c, 4 * i * NK:4 * (i + 1) * NK],
                                             start=(c == 0), stop=(c == CT - 1))
                    last.then_inc(sem["xsc"], 1)

                def x_turn(t):
                    after(pe, "xnorm", t + 1)
                    for i in range(3):
                        if 3 * t + i >= 2:
                            after(pe, "pt_out", 3 * t + i - 1)
                        for k in range(4 * i, min(4 * i + 4, PT)):
                            n = P if k < PT - 1 else LAST
                            last = pe.transpose(PS[0:n, 4 + (3 * t + i) % 2, (k % 4) * P:(k % 4 + 1) * P],
                                                prob[:, t % 3, k * P:k * P + n], ident[:, :])
                        last.then_inc(sem["ptr"], 1)

                def x_weigh(t):
                    if t == 0:
                        after(pe, "mn_in", 48)
                    after(pe, "pt_out", 3 * t + 3)
                    if t >= 2:
                        after(pe, "x_res", t - 1)
                    for k in range(PT):
                        n = P if k < PT - 1 else LAST
                        last = pe.matmul(PS[:, 6 + t % 2, 0:C], pT[0:n, t % 2, k, :], Nb[0:n, k, :],
                                         start=(k == 0), stop=(k == PT - 1))
                    last.then_inc(sem["xo"], 1)

                after(pe, "o_res", T)
                after(pe, "mn_in", 48)
                after(pe, "o_ready", G * QH)
                for t in range(T + 1):
                    if t < T:
                        x_scores(t)
                    if t >= 1:
                        x_turn(t - 1)
                        x_weigh(t - 1)
                for t in range(T):
                    transpose_x(2, t)
                after(pe, "xs", 1)
                for c in range(CT):
                    last = pe.matmul(PS[0:1, 7, 0:E], xsum[:, c:c + 1], Wr_sb[:, c, :],
                                     start=(c == 0), stop=(c == CT - 1))
                last.then_inc(sem["rsc"], 1)
                after(pe, "xt", 3 * T)
                after(pe, "pt_out", 3 * T)
                after(pe, "w_in", PER["w_in"])
                pe.transpose(PS[:, 6, 0:FT], b1_rows[:, :], ident[0:FT, 0:FT]).then_inc(sem["b1_tr"], 1)
                for f in range(2 * FT):
                    ft, half = f // 2, f % 2
                    if f >= 4:
                        after(pe, "h_out", f - 3)
                    for c in range(CT):
                        last = pe.matmul(PS[:, f % 4, :], W1_sb[:, c, ft * P:(ft + 1) * P],
                                         xT[:, c, half * 512:(half + 1) * 512], start=(c == 0), stop=(c == CT - 1))
                    last.then_inc(sem["h_prod"], 1)
                after(pe, "h_out", 2 * FT)
                for t in range(T):
                    if t >= 2:
                        after(pe, "y_res", t - 1)
                    for f in range(FT):
                        last = pe.matmul(PS[:, 4 + t % 2, 0:C], hT[:, f, t * P:(t + 1) * P], W2_sb[:, f, :],
                                         start=(f == 0), stop=(f == FT - 1))
                    last.then_inc(sem["y"], 1)
                batch_end(pe)


_INS = ['x', 'ctx_768', 'L0_attn_wq', 'L0_attn_wk', 'L0_attn_wv', 'L0_attn_wo', 'L0_xattn_Wq', 'L0_xattn_Wk',
        'L0_xattn_Wv', 'L0_xattn_Wo', 'L0_xattn_bo', 'L0_ffn_Wr', 'L0_ffn_br', 'L0_ffn_W1', 'L0_ffn_b1',
        'L0_ffn_W2', 'L0_ffn_b2']
_OUTS = [((4, 1024, 256), 'float32')]


def kernel(**inputs):
    import numpy as _np
    import concourse.bacc as _bacc
    from concourse import mybir as _mybir
    from concourse.bass_utils import run_bass_kernel_spmd as _run

    nc = _bacc.Bacc("TRN2", target_bir_lowering=False, num_devices=1)
    arrays, args = {}, []
    for name in _INS:
        a = _np.ascontiguousarray(inputs[name])
        arrays[f"in_{name}_dram"] = a
        args.append(nc.dram_tensor(f"in_{name}_dram", a.shape, _mybir.dt.from_np(a.dtype), kind="ExternalInput").ap())
    for i, (shape, dtype) in enumerate(_OUTS):
        dt = _mybir.dt.from_np(_np.dtype(dtype))
        args.append(nc.dram_tensor(f"out_{i}_dram", shape, dt, kind="ExternalOutput").ap())
    decoder_layer(nc, *args)
    r = _run(nc, [arrays], core_ids=[0])
    return r.results[0]["out_0_dram"]
```

```python
from contextlib import ExitStack

import concourse.bass as bass
from concourse import mybir

F32 = mybir.dt.float32
BF16 = mybir.dt.bfloat16
I32 = mybir.dt.int32
U32 = mybir.dt.uint32
ALU = mybir.AluOpType
ACT = mybir.ActivationFunctionType
AX = mybir.AxisListType.X

P = 128
EPS = 1e-5
NORM_MIN = 64.0
DENOM_MIN = 1e-6


def decoder_layer(nc, x, ctx_in, wq, wk, wv, wo, Wq, Wk, Wv, Wo, bo, Wr, br, W1, b1, W2, b2, out):
    B, N, C = x.shape
    H = 16
    D = C // H
    S = 32
    NK, CE = ctx_in.shape[1:]
    CEH = CE // 2
    INNER = Wq.shape[1]
    E, _, FF = W1.shape
    T = N // P
    CT = C // P
    G = H // 4
    QW = 512
    QH = N // QW
    QUADS = G * QH * T
    HP = H // 2
    FT = FF // P
    NKEY = H * NK
    PT = -(-NKEY // P)
    LAST = NKEY - (PT - 1) * P

    ctx = ExitStack()
    with ctx:
        def sb(name, shape, dt=F32):
            return ctx.enter_context(nc.sbuf_tensor(name, shape, dt))

        ident = sb("ident", [P, P])
        ident16 = sb("ident16", [P, P], BF16)
        wqkvT = sb("wqkvT", [P, CT, 3 * C])
        woT = sb("woT", [P, G, C])
        Wr_sb = sb("Wr_sb", [P, CT, E])
        br_sb = sb("br_sb", [1, E])
        bo_sb = sb("bo_sb", [P, C])
        neg_block = sb("neg_block", [P, P])
        den_pick = sb("den_pick", [P, P])
        x_raw = sb("x_raw", [P, T, C])
        x_res = sb("x_res", [P, T, C])
        x_hat = sb("x_hat", [P, T, C])
        xT = sb("xT", [P, CT, N])
        arena_a = sb("arena_a", [P, T * 2 * H * S])
        feat = arena_a[:, :].rearrange("p (w g t j s) -> p w g t j s", w=2, g=G, t=T, j=4)
        m_w = CT * NKEY
        Mb = arena_a[:, 0:m_w].rearrange("p (c k) -> p c k", c=CT)
        Nb = arena_a[:, m_w:m_w + PT * C].rearrange("p (i o) -> p i o", i=PT)
        pT = arena_a[:, m_w + PT * C:m_w + PT * C + 2 * PT * P].rearrange("p (b i q) -> p b i q", b=2, i=PT)
        v_aug = sb("v_aug", [P, T, H, S])
        NF, NS = D + 2, 6
        KR = NS * NF
        arena_b = sb("arena_b", [P, 2 * G * N])
        arena_s = sb("arena_s", [P, 7680])
        g_sums = arena_b[:, 0:G * N].rearrange("p (g n) -> p g n", g=G)
        opT = (arena_s[:, 0:G * N].bitcast(BF16).rearrange("p (w j n) -> p w j n", w=2, j=4),
               arena_b[:, G * N:2 * G * N].bitcast(BF16).rearrange("p (w j n) -> p w j n", w=2, j=4))
        n_parts = 2 * T * 4 * KR // 2
        parts = arena_s[:, G * N:G * N + n_parts].bitcast(BF16).rearrange(
            "p (w x s f) -> p w x s f", w=2, x=T * 4, s=NS)
        rest = sb("rest", [P, 2, T * 4, NF])
        hT = arena_b[:, :].rearrange("p (f n) -> p f n", f=FT)
        oT = sb("oT", [P, G, N])
        qT = oT
        NBUF = 3
        arena_t = sb("arena_t", [P, NBUF * 4 * QW])
        root = arena_t[:, :].rearrange("p (b j q) -> p b (j q)", b=NBUF, j=4)
        xT_next = arena_t[:, CT * FF + FT * C:CT * FF + FT * C + CT * N].rearrange("p (c n) -> p c n", c=CT)
        sq = arena_s[:, G * N:G * N + 2 * 2 * C].rearrange("p (b c) -> p b c", b=2)
        gen = arena_t[:, 0:6 * QW].rearrange("p (i q) -> p i q", i=6)
        g_denom, g_over, g_u, g_root, g_root2, g_weight = (gen[:, i, :] for i in range(6))
        one_minus_q = arena_t[:, 6 * QW:7 * QW].rearrange("p (j m) -> p j m", j=4)
        g_v = arena_t[:, 7 * QW:7 * QW + S]
        g_k = arena_t[:, 7 * QW + S:7 * QW + S + 1]
        Wq_nat = arena_a[:, 0:CT * INNER].rearrange("p (c i) -> p c i", c=CT)
        Wk_sb = arena_a[0:CEH, 2048:4096].rearrange("p (c i) -> p c i", c=2)
        Wv_sb = arena_a[0:CEH, 4096:6144].rearrange("p (c i) -> p c i", c=2)
        Wo_sb = arena_a[:, 6144:8192].rearrange("p (h o) -> p h o", h=HP)
        w_nat = arena_b[:, 0:3 * CT * C].rearrange("p (w c i) -> p w c i", w=3, c=CT)
        wo_pad = arena_b[:, 2048:2048 + CT * G * P].rearrange("p (c g j s) -> p c g j s", c=CT, g=G, j=4)
        WqT = arena_b[:, 4096:4096 + HP * C].rearrange("p (h c) -> p h c", h=HP)
        ctxT = arena_b[0:CEH, 6144:6144 + 2 * B * NK].rearrange("p (c b k) -> p c b k", c=2, b=B)
        ctx_sb = arena_b[0:NK, 3072:3072 + B * CE].rearrange("p (b c) -> p b c", b=B)
        kx = arena_t[:, 0:HP * B * NK].rearrange("p (h b k) -> p h b k", h=HP, b=B)
        vx = arena_t[:, HP * B * NK:2 * HP * B * NK].rearrange("p (h b k) -> p h b k", h=HP, b=B)
        prob = arena_t[:, 0:3 * NKEY].rearrange("p (b k) -> p b k", b=3)
        W1_sb = arena_t[:, 0:CT * FF].rearrange("p (c f) -> p c f", c=CT)
        W2_sb = arena_t[:, CT * FF:CT * FF + FT * C].rearrange("p (f o) -> p f o", f=FT)
        Gm = sb("Gm", [P, G, P])
        norms = sb("norms", [P, 2, G, T, 4])
        one_minus = sb("one_minus", [P, 2, G, T, 4])
        inv = sb("inv", [P, 2, G, T, 4])
        recip_den = x_hat[:, 0:QW // C, :].rearrange("p t c -> p (t c)")
        stats, meanvar, std, rstd = (sb(n, [P, 2, T, w]) for n, w in (("stats", 6), ("meanvar", 2), ("std", 1), ("rstd", 1)))
        norm_low = sb("norm_low", [P, 1])
        low1 = sb("low1", [1, 1])
        fast_flag = sb("fast_flag", [1, 1], I32)
        pmax = sb("pmax", [P, 2, H])
        psumr = sb("psumr", [P, 2, H])
        pinv = sb("pinv", [P, 2, H])
        xsum = sb("xsum", [P, CT])
        route_s = sb("route_s", [1, E])
        route_m = sb("route_m", [1, 8])
        route_i = sb("route_i", [1, 8], U32)
        b1_rows = sb("b1_rows", [FT, P])
        b1_sb = sb("b1_sb", [P, FT])
        b2_sb = sb("b2_sb", [P, C])
        n_dram = nc.dram_tensor("n_rows_dram", (B, NKEY, C), F32, kind="Internal").ap()
        m_dram = nc.dram_tensor("m_cols_dram", (B, C, NKEY), F32, kind="Internal").ap()
        n_stage = [oT[0:NK, :, :].rearrange("p g n -> p (g n)").rearrange("p (h o) -> p h o", h=H),
                   arena_s[0:NK, 0:H * C].rearrange("p (h o) -> p h o", h=H)]
        m_stage = arena_s[:, 0:B * NKEY].rearrange("p (b h k) -> p b h k", b=B, h=H)
        SETS = (("n", 0, 0), ("m", 0, 1), ("n", 1, 0), ("m", 1, 1), ("n", 2, 0), ("n", 3, 1))

        def stored_before(n, st):
            return sum(which == st for _, _, which in SETS[:n])

        PS = ctx.enter_context(nc.psum_tensor("PS", [P, 8, 512], F32))

        PER = dict(
            x_in=16, presets=4, f_stats=1, f_std=1, f_xhat=T, f_tr=T, f_xt=T,
            qk=T, v=T, squares=T, qk_out=T, norm=T, v_out=T,
            nlow=1, nlowT=1, flag=1, scaled=2,
            trq=2 * G, q_ready=2 * G, gmat=G, g_ready=G, f_split=4, f_tr6=8, f_op_ready=8,
            split=4 * (G - 1), tr6=8 * (G - 1), op_ready=8 * (G - 1),
            sc_act=QUADS, sc_dve=QUADS, squared=QUADS, z_out=QUADS, z_sq=QUADS, rooted=QUADS, pv=QUADS,
            acc_out=G * QH, den=G * QH, rden=2 * G * QH, o_ready=G * QH,
            x_res_free=1, oproj=T, o_res=T,
            stats=2, std=2, xhat=2 * T, tr=2 * T, xt=2 * T,
            mn_in=48, bo_added=1,
            xsc=T, xmax=T, shifted=T, xexp=T, xsum=T, xinv=T, xnorm=T, ptr=3 * T, pt_out=3 * T, xo=T, x_res=T,
            xs=1, rsc=1, route=1, w1_in=32, w2_in=32, b1_tr=1, b1_out=1, b2_added=1,
            h_prod=2 * FT, h_out=2 * FT, y=T, y_res=T,
            dve_step=100, batch_done=4,
        )
        sem = {k: ctx.enter_context(nc.semaphore("s_" + k)) for k in PER}
        once = {k: ctx.enter_context(nc.semaphore("s_" + k)) for k in
                ("weights", "setup", "wtr", "wtr_out", "kvx", "kvx_out", "mn", "m_out", "n_out", "stored0", "stored1")}
        SETUP_STEPS = 13
        go, gone, stored = (ctx.enter_context(nc.semaphore("s_" + k)) for k in ("go", "gone", "stored"))
        hand = {k: ctx.enter_context(nc.semaphore("s_gen_" + k)) for k in
                ("start", "products", "u", "roots", "weights", "sums")}
        first, last_sem = sem["x_in"].num, sem["batch_done"].num
        assert last_sem - first == len(sem) - 1

        def after(eng, name, n):
            assert 0 < n <= PER[name]
            eng.wait_ge(sem[name], n)

        def all_batches(eng, batch):
            with eng.Fori(0, B - 1) as b:
                batch(b, b + 1)
            batch(B - 1, None)

        def batch_end(eng):
            eng.drain().then_inc(sem["batch_done"], 1)
            eng.wait_ge(go, 1)
            eng.sem_inc(gone, 1)

        def take(eng, name):
            eng.wait_ge(hand[name], 1)
            eng.sem_clear(hand[name])

        def every_key_tile(eng, body):
            with eng.Fori(0, QH) as qh:
                with eng.Fori(0, T) as kt:
                    for j in range(4):
                        body(qh, kt, j)

        def load_flag(eng):
            return eng.value_load(fast_flag[0:1, 0:1], min_val=0, max_val=1)

        SIDE = {f: [("qT", 2 * f - 12), ("qT", 2 * f - 11)] for f in range(6, 10)}
        SIDE.update({f: [("Gm", f - 10)] for f in range(10, 14)})

        N_WEIGHT_DMAS = 3 + CT * G + 1 + 2 + 1 + 3 + 1

        block = ctx.enter_context(nc.Block())

        @block.sync
        def _(sp):
            for i, w in enumerate((wq, wk, wv)):
                sp.dma_start(w_nat[:, i], w.rearrange("(c p) i -> p c i", p=P)).then_inc(once["weights"], 16)
            sp.wait_ge(once["setup"], 1)
            for c in range(CT):
                for g in range(G):
                    sp.dma_start(wo_pad[:, c, g, :, 0:D], wo[c * P:(c + 1) * P, g * 4 * D:(g + 1) * 4 * D]
                                 .rearrange("p (j d) -> p j d", j=4)).then_inc(once["weights"], 16)
            sp.dma_start(Wq_nat, Wq.rearrange("(c p) i -> p c i", p=P)).then_inc(once["weights"], 16)
            for dst, w in ((Wk_sb, Wk), (Wv_sb, Wv)):
                sp.dma_start(dst, w.rearrange("(c p) i -> p c i", p=CEH)).then_inc(once["weights"], 16)
            sp.dma_start(Wo_sb, Wo.rearrange("(h p) o -> p h o", p=P)).then_inc(once["weights"], 16)
            sp.dma_start(Wr_sb[:, :, :], Wr.rearrange("(c p) e -> p c e", p=P)).then_inc(once["weights"], 16)
            sp.dma_start(br_sb[:, :], br.rearrange("(a e) -> a e", a=1)).then_inc(once["weights"], 16)
            sp.dma_start(bo_sb[:, :], bo.rearrange("(a c) -> a c", a=1).to_broadcast([P, C])).then_inc(once["weights"], 16)
            sp.dma_start(ctx_sb, ctx_in.rearrange("b k c -> k b c")).then_inc(once["weights"], 16)
            done_n, done_m = 0, 0
            for kind, i, st in SETS:
                if kind == "n":
                    done_n += H // 2
                    sp.wait_ge(once["n_out"], done_n)
                    sp.dma_start(n_dram[i].rearrange("(h k) o -> k h o", h=H), n_stage[st]).then_inc(once[f"stored{st}"], 16)
                else:
                    done_m += H
                    sp.wait_ge(once["m_out"], done_m)
                    sp.dma_start(m_dram[:, i * P:(i + 1) * P, :].rearrange("b p k -> p b k"),
                                 m_stage.rearrange("p b h k -> p b (h k)")).then_inc(once["stored1"], 16)
            for st in range(2):
                sp.wait_ge(once[f"stored{st}"], 16 * stored_before(len(SETS), st))
            def load_x(b):
                sp.dma_start(x_raw[:, :, :], x[bass.ds(b, 1)].rearrange("a (t p) c -> p (a t) c", p=P)
                             ).then_inc(sem["x_in"], 16)

            def all_meet():
                after(sp, "batch_done", 4)
                sp.sem_clear(range(first, last_sem + 1))
                sp.sem_inc(go, 1)
                sp.wait_ge(gone, 4)
                sp.sem_clear(go)
                sp.sem_clear(gone)

            def batch(b, nxt):
                sp.wait_ge(stored, 32)
                sp.sem_clear(stored)
                sp.sem_inc(sem["x_res_free"], 1)
                after(sp, "split", PER["split"])
                sp.dma_start(Mb, m_dram[bass.ds(b, 1)].rearrange("a (c p) k -> p (a c) k", p=P)).then_inc(sem["mn_in"], 16)
                sp.dma_start(Nb[:, 0:PT - 1, :], n_dram[bass.ds(b, 1), 0:(PT - 1) * P, :]
                             .rearrange("a (i p) o -> p (a i) o", p=P)).then_inc(sem["mn_in"], 16)
                sp.dma_start(Nb[0:LAST, PT - 1, :], n_dram[bass.ds(b, 1), (PT - 1) * P:NKEY, :]
                             .rearrange("a p o -> (a p) o")).then_inc(sem["mn_in"], 16)
                if nxt is not None:
                    after(sp, "o_res", T)
                    load_x(nxt)
                after(sp, "route", 1)
                e = sp.value_load(route_i[0:1, 0:1], min_val=0, max_val=E - 1)
                sp.dma_start(W1_sb, W1[bass.ds(e, 1)].rearrange("a (c p) f -> p (a c) f", p=P)).then_inc(sem["w1_in"], 16)
                sp.dma_start(b1_rows[:, :], b1[bass.ds(e, 1)].rearrange("a (f p) -> (a f) p", p=P)).then_inc(sem["w1_in"], 16)
                sp.dma_start(b2_sb[:, :], b2[bass.ds(e, 1)].to_broadcast([P, C])).then_inc(sem["w2_in"], 16)
                sp.dma_start(W2_sb, W2[bass.ds(e, 1)].rearrange("a (f p) o -> p (a f) o", p=P)).then_inc(sem["w2_in"], 16)
                for half in range(2):
                    t0 = half * T // 2
                    after(sp, "y_res", t0 + T // 2)
                    sp.dma_start(out[bass.ds(b, 1)].rearrange("a (t p) c -> p (a t) c", p=P)[:, t0:t0 + T // 2],
                                 x_res[:, t0:t0 + T // 2, :]).then_inc(stored, 16)
                all_meet()

            load_x(0)
            all_meet()
            sp.sem_inc(stored, 32)
            all_batches(sp, batch)
            sp.wait_ge(stored, 32)

        @block.gpsimd
        def _(pool):
            done = [0]

            def setup(ins):
                done[0] += 1
                ins.then_inc(once["setup"], 1)
                pool.wait_ge(once["setup"], done[0])

            setup(pool.memset(wo_pad, 0.0))
            setup(pool.memset(ident[:, :], 0.0))
            setup(pool.affine_select(out=ident[:, :], in_=ident[:, :], compare_op=ALU.not_equal, fill=1.0,
                                     base=0, pattern=[[-1, P]], channel_multiplier=1))
            setup(pool.tensor_copy(ident16[:, :], ident[:, :]))
            setup(pool.memset(den_pick[:, :], 0.0))
            pick = den_pick[:, :].rearrange("p (j m) -> p j m", j=4)
            setup(pool.affine_select(out=pick, in_=pick, compare_op=ALU.not_equal, fill=1.0, base=-D,
                                     pattern=[[-S, 4], [0, S]], channel_multiplier=1))
            setup(pool.memset(neg_block[:, :], 0.0))
            for j in range(4):
                setup(pool.memset(neg_block[j * S:(j + 1) * S, j * S:(j + 1) * S], -1.0))
            setup(pool.memset(v_aug[:, :, :, D:S].rearrange("p t h s -> p (t h) s"), 0.0))
            setup(pool.memset(v_aug[:, :, :, D:D + 1].rearrange("p t h s -> p (t h) s"), 1.0))
            assert done[0] == SETUP_STEPS
            pool.wait_ge(once["m_out"], 2 * H)
            pool.wait_ge(once["n_out"], B * H // 2)
            def front():
                flat = feat.rearrange("p w g t j s -> p (w g t j) s")
                half = flat.shape[1] // 2
                presets = ((flat[:, :, D + 3:S], 0.0), (flat[:, :, D + 2:D + 3], 1.0),
                           (flat[:, 0:half, D + 1:D + 2], 1.0), (flat[:, half:2 * half, D:D + 1], 2.0))
                for i, (places, value) in enumerate(presets):
                    pool.memset(places, value).then_inc(sem["presets"], 1)
                    after(pool, "presets", i + 1)

            def batch(b, nxt):
                fast = load_flag(pool)
                with pool.If(fast == 1):
                    for q in range(QUADS):
                        after(pool, "z_out", q + 1)
                        zt = root[:, q % NBUF, 2 * QW:4 * QW]
                        pool.tensor_tensor(zt, zt, zt, ALU.mult).then_inc(sem["z_sq"], 1)
                after(pool, "xhat", T)
                pool.tensor_tensor(x_res[:, :, :], x_res[:, :, :],
                                   bo_sb[:, None, :].to_broadcast([P, T, C]), ALU.add).then_inc(sem["bo_added"], 1)
                if nxt is not None:
                    after(pool, "xo", T)
                    front()
                after(pool, "xhat", 2 * T)
                after(pool, "w2_in", PER["w2_in"])
                pool.tensor_tensor(x_res[:, :, :], x_res[:, :, :],
                                   b2_sb[:, None, :].to_broadcast([P, T, C]), ALU.add).then_inc(sem["b2_added"], 1)
                batch_end(pool)

            front()
            batch_end(pool)
            all_batches(pool, batch)

        @block.scalar
        def _(act):
            for i in range(3):
                act.wait_ge(once["wtr"], i + 1)
                act.activation(wqkvT[:, :, i * C:(i + 1) * C], PS[:, i, :].rearrange("p (c o) -> p c o", c=CT),
                               ACT.Copy).then_inc(once["wtr_out"], 1)
            for i in range(2):
                act.wait_ge(once["wtr"], 4 + i)
                act.activation(woT[:, 2 * i:2 * i + 2, :], PS[:, 3 + i, :].rearrange("p (g o) -> p g o", g=2),
                               ACT.Copy).then_inc(once["wtr_out"], 1)
            for i in range(4):
                act.wait_ge(once["wtr"], 6 + i)
                act.activation(WqT[:, 2 * i:2 * i + 2, :], PS[:, (5 + i) % 8, :].rearrange("p (g o) -> p g o", g=2),
                               ACT.Copy).then_inc(once["wtr_out"], 1)
            for c in range(2):
                act.wait_ge(once["wtr"], 10 + c)
                act.activation(ctxT[:, c], PS[0:CEH, 1 + c, 0:B * NK].rearrange("p (b k) -> p b k", b=B), ACT.Copy
                               ).then_inc(once["wtr_out"], 1)
            for i in range(2 * HP):
                act.wait_ge(once["kvx"], i + 1)
                act.activation((kx, vx)[i // HP][:, i % HP], PS[:, i % 4, 0:B * NK].rearrange("p (b k) -> p b k", b=B),
                               ACT.Copy).then_inc(once["kvx_out"], 1)
            at, stored = 0, 0
            for n, (kind, i, st) in enumerate(SETS):
                if kind == "m":
                    at += H
                    continue
                if stored_before(n, st):
                    act.wait_ge(once[f"stored{st}"], 16 * stored_before(n, st))
                for k in range(H // 2):
                    at += 1
                    act.wait_ge(once["mn"], at)
                    heads = 4 * (k // 2) + k % 2
                    act.activation(n_stage[st][:, heads:heads + 3:2, :],
                                   PS[0:NK, 4 + k % 4, :].rearrange("p (h o) -> p h o", h=2), ACT.Copy
                                   ).then_inc(once["n_out"], 1)

            def layer_norm_std(i):
                after(act, "stats", i + 1)
                act.activation(std[:, 0, :, 0], meanvar[:, 0, :, 1], ACT.Sqrt, bias=EPS).then_inc(sem["std"], 1)

            def xT_out(i, t):
                after(act, "tr", i * T + t + 1)
                act.activation(xT[:, :, t * P:(t + 1) * P], PS[:, t % 2, 0:C].rearrange("p (c n) -> p c n", c=CT),
                               ACT.Copy).then_inc(sem["xt"], 1)

            def front_std():
                after(act, "f_stats", 1)
                act.activation(std[:, 1, :, 0], meanvar[:, 1, :, 1], ACT.Sqrt, bias=EPS).then_inc(sem["f_std"], 1)

            def front_transposed():
                for t in range(T):
                    after(act, "f_tr", t + 1)
                    act.activation(xT_next[:, :, t * P:(t + 1) * P], PS[:, t % 2, 0:C].rearrange("p (c n) -> p c n", c=CT),
                                   ACT.Copy).then_inc(sem["f_xt"], 1)

            def front_projected():
                for t in range(T):
                    after(act, "qk", t + 1)
                    if t >= 2:
                        after(act, "norm", t - 1)
                    src = PS[:, 2 + t % 2, :]
                    act.activation(sq[:, t % 2, :], src, ACT.Square).then_inc(sem["squares"], 1)
                    if t == 0:
                        after(act, "presets", 4)
                    act.activation(feat[:, 0, :, t, :, 0:D], src[:, 0:C].rearrange("p (g j d) -> p g j d", g=G, j=4), ACT.Copy)
                    act.activation(feat[:, 1, :, t, :, 0:D], src[:, C:2 * C].rearrange("p (g j d) -> p g j d", g=G, j=4),
                                   ACT.Copy, scale=-4.0).then_inc(sem["qk_out"], 1)

            def front_qT(f):
                g, half = f // 2, f % 2
                after(act, "trq", f + 1)
                act.activation(qT[:, g, half * 512:(half + 1) * 512], PS[:, 6 + f % 2, :], ACT.Copy
                               ).then_inc(sem["q_ready"], 1)

            def batch(b, nxt):
                def square(q):
                    after(act, "sc_act", q + 1)
                    if q >= NBUF:
                        after(act, "pv", q - NBUF + 1)
                    act.activation(root[:, q % NBUF, 0:2 * QW],
                                   PS[:, 2 * (q % 2):2 * (q % 2) + 2, :].rearrange("p j q -> p (j q)"),
                                   ACT.Square, bias=1.0).then_inc(sem["squared"], 1)

                def take_root(q):
                    after(act, "squared", q + 1)
                    after(act, "z_sq", q + 1)
                    act.activation(root[:, q % NBUF, :], root[:, q % NBUF, :], ACT.Sqrt, bias=-1.0
                                   ).then_inc(sem["rooted"], 1)

                def general_roots(qh, kt, j):
                    take(act, "u")
                    act.activation(g_root, g_u, ACT.Sqrt)
                    act.activation(g_root2, g_u, ACT.Sqrt, bias=2.0).then_inc(hand["roots"], 1)

                fast = load_flag(act)
                with act.If(fast == 1):
                    for q in range(QUADS):
                        square(q)
                        if q >= 1:
                            take_root(q - 1)
                    take_root(QUADS - 1)
                with act.Else():
                    for g in range(G):
                        every_key_tile(act, general_roots)

                layer_norm_std(0)
                for t in range(T):
                    xT_out(0, t)

                def p_out(t, i):
                    n = min(4, PT - 4 * i)
                    after(act, "ptr", 3 * t + i + 1)
                    act.activation(pT[:, t % 2, 4 * i:4 * i + n, :],
                                   PS[:, 4 + (3 * t + i) % 2, 0:n * P].rearrange("p (i q) -> p i q", i=n), ACT.Copy
                                   ).then_inc(sem["pt_out"], 1)

                for t in range(T + 1):
                    if t == T and nxt is not None:
                        front_std()
                    if t >= 1:
                        if t >= 3:
                            after(act, "xo", t - 2)
                        for i in range(3):
                            p_out(t - 1, i)
                    if t < T:
                        after(act, "shifted", t + 1)
                        act.activation(prob[:, t % 3, :], prob[:, t % 3, :], ACT.Exp).then_inc(sem["xexp"], 1)
                if nxt is not None:
                    front_transposed()
                layer_norm_std(1)
                for t in range(T):
                    xT_out(1, t)
                if nxt is not None:
                    front_projected()
                after(act, "b1_tr", 1)
                act.activation(b1_sb[:, :], PS[:, 6, 0:FT], ACT.Copy).then_inc(sem["b1_out"], 1)
                after(act, "b1_out", 1)
                for f in range(2 * FT):
                    after(act, "h_prod", f + 1)
                    act.activation(hT[:, f // 2, (f % 2) * 512:(f % 2 + 1) * 512], PS[:, f % 4, :], ACT.Relu,
                                   bias=b1_sb[:, f // 2:f // 2 + 1]).then_inc(sem["h_out"], 1)
                    if nxt is not None:
                        for kind, i in SIDE.get(f, ()):
                            if kind == "qT":
                                front_qT(i)
                batch_end(act)

            front_std()
            front_transposed()
            front_projected()
            for f in range(2 * G):
                front_qT(f)
            batch_end(act)
            all_batches(act, batch)

        @block.vector
        def _(dve):
            at = 0
            for n, (kind, i, st) in enumerate(SETS):
                if kind == "n":
                    at += H // 2
                    continue
                if stored_before(n, st):
                    dve.wait_ge(once[f"stored{st}"], 16 * stored_before(n, st))
                for k in range(H):
                    at += 1
                    dve.wait_ge(once["mn"], at)
                    dve.tensor_scalar(m_stage[:, :, k, :], PS[:, k % 4, 0:B * NK].rearrange("p (b k) -> p b k", b=B),
                                      float(INNER // H) ** -0.5, None, ALU.mult).then_inc(once["m_out"], 1)
            steps = [0]

            def step(ins):
                steps[0] += 1
                ins.then_inc(sem["dve_step"], 1)
                after(dve, "dve_step", steps[0])

            def tile_stats(src, t, of_next=0):
                return dve.bn_stats(stats[:, of_next, t, :], src[:, t, :])

            def layer_norm(src, names, i=0, of_next=0, x_hat_free=None):
                at_stats, at_std, at_xhat = names
                mv, r_std = meanvar[:, of_next], rstd[:, of_next]
                for t in range(T):
                    ins = dve.bn_aggr(mv[:, t, :], stats[:, of_next, t, :])
                    if t == T - 1:
                        ins.then_inc(sem[at_stats], 1)
                after(dve, at_std, i + 1)
                step(dve.reciprocal(r_std[:, :, 0], std[:, of_next, :, 0]))
                if x_hat_free:
                    after(dve, *x_hat_free)
                for t in range(T):
                    dve.tensor_scalar(x_hat[:, t, :], src[:, t, :], mv[:, t, 0:1], r_std[:, t, :],
                                      ALU.subtract, ALU.mult).then_inc(sem[at_xhat], 1)

            def front_stats(tiles):
                after(dve, "x_in", 16)
                for t in tiles:
                    ins = tile_stats(x_raw, t, of_next=1)
                    if t == T - 1:
                        step(ins)

            def front_norm(x_hat_free=None):
                layer_norm(x_raw, ("f_stats", "f_std", "f_xhat"), of_next=1, x_hat_free=x_hat_free)

            norms_flat, om_flat, inv_flat = (a[:, :, :, :, :].rearrange("p w g t j -> p (w g t j)")
                                             for a in (norms, one_minus, inv))
            half_n = T * H
            flat = feat.rearrange("p w g t j s -> p (w g t j) s")

            def front_features():
                for t in range(T):
                    after(dve, "squares", t + 1)
                    dve.tensor_reduce(norms[:, :, :, t, :].rearrange("p w g j -> p (w g) j"),
                                      sq[:, t % 2, :].rearrange("p (h j d) -> p h j d", j=4, d=D), AX, ALU.add
                                      ).then_inc(sem["norm"], 1)
                    after(dve, "v", t + 1)
                    dve.tensor_copy(v_aug[:, t, :, 0:D], PS[:, 4 + t % 2, 0:C].rearrange("p (h d) -> p h d", h=H)
                                    ).then_inc(sem["v_out"], 1)
                after(dve, "norm", T)
                dve.tensor_reduce(norm_low[:, :], norms_flat, AX, ALU.min
                                  ).then_inc(sem["nlow"], 1)
                step(dve.tensor_scalar(om_flat, norms_flat, -1.0, 1.0, ALU.mult, ALU.add))
                step(dve.reciprocal(inv_flat, om_flat))
                after(dve, "presets", 4)
                dve.tensor_copy(flat[:, 0:half_n, D], norms_flat[:, 0:half_n])
                step(dve.tensor_scalar(flat[:, half_n:2 * half_n, D + 1], norms_flat[:, half_n:2 * half_n], 2.0, None, ALU.mult))
                after(dve, "nlowT", 1)
                step(dve.tensor_reduce(low1[:, :], PS[0:1, 6, 0:P], AX, ALU.min))
                dve.tensor_scalar(fast_flag[:, :], low1[:, :], NORM_MIN, None, ALU.is_ge).then_inc(sem["flag"], 1)
                after(dve, "flag", 1)
                with dve.If(load_flag(dve) == 0):
                    dve.memset(inv_flat, 1.0)
                    dve.drain()
                after(dve, "qk_out", T)
                for w in range(2):
                    part = flat[:, w * half_n:(w + 1) * half_n, 0:NF]
                    dve.tensor_tensor(part, part, inv_flat[:, w * half_n:(w + 1) * half_n, None]
                                      .to_broadcast([P, half_n, NF]), ALU.mult).then_inc(sem["scaled"], 1)
                after(dve, "scaled", 2)

            def group(g):
                return feat[:, :, g, :, :, 0:NF].rearrange("p w t j s -> p w (t j) s")

            def high_q(g):
                f = group(g)[:, 0]
                dve.tensor_copy(parts[:, 0, :, 0:4:3, :], f[:, :, None, :].to_broadcast([P, T * 4, 2, NF])
                                ).then_inc(sem["dve_step"], 1)
                dve.tensor_copy(parts[:, 0, :, 5, :], f).then_inc(sem["dve_step"], 1)
                steps[0] += 2

            def high_k(g):
                f = group(g)[:, 1]
                step(dve.tensor_copy(parts[:, 1, :, 0:3, :], f[:, :, None, :].to_broadcast([P, T * 4, 3, NF])))

            def less_high(g):
                step(dve.tensor_tensor(rest[:, :, :, :], group(g), parts[:, :, :, 0, :], ALU.subtract))

            def middle(g):
                name, base = ("split", 4 * (g - 1)) if g else ("f_split", 0)
                dve.tensor_copy(parts[:, 0, :, 1:5:3, :], rest[:, 0, :, None, :].to_broadcast([P, T * 4, 2, NF])
                                ).then_inc(sem[name], 1)
                dve.tensor_copy(parts[:, 1, :, 3:5, :], rest[:, 1, :, None, :].to_broadcast([P, T * 4, 2, NF])
                                ).then_inc(sem[name], 1)
                after(dve, name, base + 2)

            def low(g):
                for w, m, l in ((0, 1, 2), (1, 3, 5)):
                    dve.tensor_tensor(parts[:, w, :, l, :], rest[:, w], parts[:, w, :, m, :], ALU.subtract
                                      ).then_inc(sem["split" if g else "f_split"], 1)

            def operand_out(g, e):
                turned, ready, base = ("tr6", "op_ready", 8 * (g - 1)) if g else ("f_tr6", "f_op_ready", 0)
                after(dve, turned, base + e + 1)
                dve.tensor_copy(opT[g % 2][0:KR, e // 4, e % 4, :], PS[0:KR, 7, :].bitcast(BF16)
                                ).then_inc(sem[ready], 1)

            def front_parts():
                high_q(0)
                high_k(0)
                less_high(0)
                middle(0)
                low(0)
                for g in range(G):
                    after(dve, "gmat", g + 1)
                    dve.tensor_tensor(Gm[:, g, :], PS[:, 6 + g % 2, 0:P], neg_block[:, :], ALU.mult
                                      ).then_inc(sem["g_ready"], 1)

            def batch(b, nxt):
                steps[0] = 0

                def acc_out(i):
                    g, qh = i // QH, i % QH
                    after(dve, "pv", T * (i + 1))
                    dve.tensor_copy(oT[:, g, qh * QW:(qh + 1) * QW], PS[:, 6, :]).then_inc(sem["acc_out"], 1)

                def recip(i, part):
                    if part == 0:
                        after(dve, "den", i + 1)
                        if i:
                            after(dve, "o_ready", i)
                    cols = slice(part * QW // 2, (part + 1) * QW // 2)
                    dve.reciprocal(recip_den[:, cols], PS[:, 7, cols]).then_inc(sem["rden"], 1)

                def normalise(i):
                    g, qh = i // QH, i % QH
                    after(dve, "rden", 2 * i + 2)
                    part = oT[:, g, qh * QW:(qh + 1) * QW]
                    dve.tensor_tensor(part, part, recip_den, ALU.mult).then_inc(sem["o_ready"], 1)

                def general_weights(g):
                    def body(qh, kt, j):
                        take(dve, "products")
                        dve.tensor_copy(g_k, one_minus[:, 1, g, bass.ds(kt, 1), j])
                        dve.tensor_copy(g_v, v_aug[:, bass.ds(kt, 1), 4 * g + j, :].rearrange("p a s -> p (a s)"))
                        dve.drain()
                        dve.tensor_scalar(g_denom, PS[:, 1, :], g_k, DENOM_MIN, ALU.mult, ALU.max)
                        dve.drain()
                        dve.reciprocal(g_over, g_denom)
                        dve.drain()
                        dve.scalar_tensor_tensor(g_u, PS[:, 0, :], 0.0, g_over, ALU.max, ALU.mult
                                                 ).then_inc(hand["u"], 1)
                        take(dve, "roots")
                        dve.tensor_tensor(g_root, g_root, g_root2, ALU.mult)
                        dve.drain()
                        dve.scalar_tensor_tensor(g_root, g_u, 1.0, g_root, ALU.add, ALU.add)
                        dve.drain()
                        dve.reciprocal(g_weight, g_root).then_inc(hand["weights"], 1)
                        take(dve, "sums")
                        rows = slice(j * S, (j + 1) * S)
                        total = g_sums[rows, g, bass.ds(qh * QW, QW)]
                        dve.tensor_tensor(total, PS[rows, 6, :], total, ALU.add).then_inc(hand["start"], 1)
                    return body

                steps_before = steps[0]
                fast = load_flag(dve)
                with dve.If(fast == 1):
                    for q in range(QUADS):
                        after(dve, "sc_dve", q + 1)
                        if q >= NBUF:
                            after(dve, "pv", q - NBUF + 1)
                        dve.tensor_scalar(root[:, q % NBUF, 2 * QW:4 * QW],
                                          PS[:, 4:6, :].rearrange("p j q -> p (j q)"), 0.0, 1.0, ALU.max, ALU.add
                                          ).then_inc(sem["z_out"], 1)
                        at, g = q % (QH * T), q // (QH * T)
                        prev = g * QH - 2
                        if q >= T and q % T == 1:
                            acc_out(q // T - 1)
                        if g:
                            if at in (0, 1):
                                recip(prev, at)
                            if at in (3, 4):
                                recip(prev + 1, at - 3)
                            if at in (2, 5):
                                normalise(prev + (at == 5))
                        if g + 1 < G:
                            for when, make in ((2, high_q), (5, high_k), (6, less_high), (7, middle), (7, low)):
                                if at == when:
                                    make(g + 1)
                            if at >= 8:
                                operand_out(g + 1, at - 8)
                    for i in (G * QH - 2, G * QH - 1):
                        if i % 2:
                            acc_out(i)
                        recip(i, 0)
                        recip(i, 1)
                        normalise(i)
                with dve.Else():
                    steps_fast, steps[0] = steps[0], steps_before
                    columns = ident[:, :].rearrange("p (j s) -> p j s", j=4)
                    dve.tensor_tensor(one_minus_q, columns[:, :, D + 1, None].to_broadcast([P, 4, P]),
                                      columns[:, :, D, None].to_broadcast([P, 4, P]), ALU.subtract)
                    dve.memset(g_sums, 0.0)
                    dve.drain().then_inc(hand["start"], 1)
                    for g in range(G):
                        if g:
                            high_q(g)
                            high_k(g)
                            less_high(g)
                            middle(g)
                            low(g)
                            for e in range(8):
                                operand_out(g, e)
                        every_key_tile(dve, general_weights(g))
                    dve.drain()
                    dve.tensor_copy(oT[:, :, :], g_sums)
                    dve.drain().then_inc(sem["acc_out"], G * QH)
                    for i in range(G * QH):
                        recip(i, 0)
                        recip(i, 1)
                        normalise(i)
                    assert steps[0] == steps_fast

                after(dve, "x_res_free", 1)
                for t in range(T):
                    after(dve, "oproj", t + 1)
                    dve.tensor_tensor(x_res[:, t, :], PS[:, 4 + t % 2, 0:C], x_raw[:, t, :], ALU.add
                                      ).then_inc(sem["o_res"], 1)
                    if t >= 1:
                        after(dve, "o_res", t)
                        tile_stats(x_res, t - 1)
                after(dve, "o_res", T)
                step(tile_stats(x_res, T - 1))
                layer_norm(x_res, ("stats", "std", "xhat"))
                def sc(t):
                    return PS[:, 0:4, 0:4 * NK].rearrange("p c (h k) -> p c h k", h=4)

                def x_sum(t):
                    after(dve, "xexp", t + 1)
                    pr = prob[:, t % 3, :].rearrange("p (h k) -> p h k", h=H)
                    dve.tensor_reduce(psumr[:, t % 2, :], pr, AX, ALU.add).then_inc(sem["xsum"], 1)
                    after(dve, "xsum", t + 1)
                    dve.reciprocal(pinv[:, t % 2, :], psumr[:, t % 2, :]).then_inc(sem["xinv"], 1)
                    after(dve, "xinv", t + 1)
                    dve.tensor_tensor(pr, pr, pinv[:, t % 2, :, None].to_broadcast([P, H, NK]), ALU.mult
                                      ).then_inc(sem["xnorm"], 1)

                def x_residual(t):
                    after(dve, "xo", t + 1)
                    if t == 0:
                        after(dve, "bo_added", 1)
                    dve.tensor_tensor(x_res[:, t, :], PS[:, 6 + t % 2, 0:C], x_res[:, t, :], ALU.add
                                      ).then_inc(sem["x_res"], 1)
                    after(dve, "x_res", t + 1)
                    return tile_stats(x_res, t)

                for t in range(T):
                    after(dve, "xsc", t + 1)
                    dve.tensor_reduce(pmax[:, t % 2, :].rearrange("p (c h) -> p c h", c=4), sc(t), AX, ALU.max
                                      ).then_inc(sem["xmax"], 1)
                    after(dve, "xmax", t + 1)
                    if t >= 3:
                        after(dve, "ptr", 3 * (t - 2))
                    dve.tensor_tensor(prob[:, t % 3, :].rearrange("p (c h k) -> p c h k", c=4, h=4), sc(t),
                                      pmax[:, t % 2, :].rearrange("p (c h) -> p c h", c=4)[:, :, :, None]
                                      .to_broadcast([P, 4, 4, NK]), ALU.subtract).then_inc(sem["shifted"], 1)
                    if t >= 3:
                        x_residual(t - 3)
                    if nxt is not None and t >= T // 2:
                        front_stats(range(2 * (t - T // 2), 2 * (t - T // 2) + 2))
                    x_sum(t)
                x_residual(T - 3)
                if nxt is not None:
                    front_norm(("tr", T))
                x_residual(T - 2)
                step(x_residual(T - 1))
                layer_norm(x_res, ("stats", "std", "xhat"), i=1,
                           x_hat_free=("tr", T) if nxt is None else ("f_tr", T))
                after(dve, "xt", 2 * T)
                dve.tensor_reduce(xsum[:, :], xT[:, :, :], AX, ALU.add).then_inc(sem["xs"], 1)
                after(dve, "rsc", 1)
                step(dve.scalar_tensor_tensor(route_s[:, :], PS[0:1, 7, 0:E], 1.0 / N, br_sb[:, :], ALU.mult, ALU.add))
                step(dve.max(route_m[:, :], route_s[:, :]))
                dve.max_index(route_i[:, :], route_m[:, :], route_s[:, :]).then_inc(sem["route"], 1)
                if nxt is not None:
                    front_features()
                    front_parts()
                after(dve, "b2_added", 1)
                for t in range(T):
                    if nxt is not None:
                        operand_out(0, t)
                    after(dve, "y", t + 1)
                    dve.tensor_tensor(x_res[:, t, :], PS[:, 4 + t % 2, 0:C], x_res[:, t, :], ALU.add
                                      ).then_inc(sem["y_res"], 1)
                batch_end(dve)

            dve.wait_ge(once["setup"], SETUP_STEPS)
            front_stats(range(T))
            front_norm()
            front_features()
            front_parts()
            for e in range(8):
                operand_out(0, e)
            batch_end(dve)
            all_batches(dve, batch)

        @block.tensor
        def _(pe):
            pe.wait_ge(once["setup"], SETUP_STEPS)
            pe.wait_ge(once["weights"], 16 * N_WEIGHT_DMAS)
            for i in range(3):
                for c in range(CT):
                    for o in range(CT):
                        last = pe.transpose(PS[:, i, c * C + o * P:c * C + (o + 1) * P],
                                            w_nat[:, i, o, c * P:(c + 1) * P], ident[:, :])
                last.then_inc(once["wtr"], 1)
            for i in range(2):
                for g in (2 * i, 2 * i + 1):
                    for o in range(CT):
                        last = pe.transpose(PS[:, 3 + i, (g % 2) * C + o * P:(g % 2) * C + (o + 1) * P],
                                            wo_pad[:, o, g].rearrange("p j s -> p (j s)"), ident[:, :])
                last.then_inc(once["wtr"], 1)
            for i in range(4):
                if i == 3:
                    pe.wait_ge(once["wtr_out"], 1)
                for h in (2 * i, 2 * i + 1):
                    for c in range(CT):
                        last = pe.transpose(PS[:, (5 + i) % 8, (h % 2) * C + c * P:(h % 2) * C + (c + 1) * P],
                                            Wq_nat[:, c, h * P:(h + 1) * P], ident[:, :])
                last.then_inc(once["wtr"], 1)
            pe.wait_ge(once["wtr_out"], 3)
            for c in range(2):
                for b in range(B):
                    last = pe.transpose(PS[0:CEH, 1 + c, b * NK:(b + 1) * NK], ctx_sb[:, b, c * CEH:(c + 1) * CEH],
                                        ident[0:NK, 0:NK])
                last.then_inc(once["wtr"], 1)
            pe.wait_ge(once["wtr_out"], 11)
            for i in range(2 * HP):
                if i >= 4:
                    pe.wait_ge(once["kvx_out"], i - 3)
                w, hp = (Wk_sb, Wv_sb)[i // HP], i % HP
                for c in range(2):
                    last = pe.matmul(PS[:, i % 4, 0:B * NK], w[:, c, hp * P:(hp + 1) * P],
                                     ctxT[:, c].rearrange("p b k -> p (b k)"), start=(c == 0), stop=(c == 1))
                last.then_inc(once["kvx"], 1)
            pe.wait_ge(once["kvx_out"], 2 * HP)
            n_done, m_done = 0, 0
            for kind, i, st in SETS:
                if kind == "n":
                    for k in range(H // 2):
                        if n_done >= 4:
                            pe.wait_ge(once["n_out"], n_done - 3)
                        odd = k % 2
                        for h in range(2):
                            hp = 2 * (k // 2) + h
                            last = pe.matmul(PS[0:NK, 4 + k % 4, h * C:(h + 1) * C],
                                             vx[64 * odd:64 * odd + 64, hp, i, :], Wo_sb[64 * odd:64 * odd + 64, hp, :],
                                             start=True, stop=True)
                        last.then_inc(once["mn"], 1)
                        n_done += 1
                else:
                    for h in range(H):
                        if m_done >= 4:
                            pe.wait_ge(once["m_out"], m_done - 3)
                        odd = h % 2
                        pe.matmul(PS[:, h % 4, 0:B * NK], WqT[64 * odd:64 * odd + 64, h // 2, i * P:(i + 1) * P],
                                  kx[64 * odd:64 * odd + 64, h // 2].rearrange("p b k -> p (b k)"),
                                  start=True, stop=True).then_inc(once["mn"], 1)
                        m_done += 1
            pe.wait_ge(once["m_out"], 2 * H)
            pe.wait_ge(once["n_out"], B * H // 2)

            def transpose_x(i, t):
                after(pe, "xhat", i * T + t + 1)
                if i * T + t >= 2:
                    after(pe, "xt", i * T + t - 1)
                for c in range(CT):
                    last = pe.transpose(PS[:, t % 2, c * P:(c + 1) * P], x_hat[:, t, c * P:(c + 1) * P], ident[:, :])
                last.then_inc(sem["tr"], 1)

            def front_transposes():
                for t in range(T):
                    after(pe, "f_xhat", t + 1)
                    if t >= 2:
                        after(pe, "f_xt", t - 1)
                    for c in range(CT):
                        last = pe.transpose(PS[:, t % 2, c * P:(c + 1) * P], x_hat[:, t, c * P:(c + 1) * P], ident[:, :])
                    last.then_inc(sem["f_tr"], 1)

            def front_project():
                for t in range(T):
                    after(pe, "f_xt", t + 1)
                    if t >= 2:
                        after(pe, "qk_out", t - 1)
                    for c in range(CT):
                        last = pe.matmul(PS[:, 2 + t % 2, :], xT_next[:, c, t * P:(t + 1) * P], wqkvT[:, c, 0:2 * C],
                                         start=(c == 0), stop=(c == CT - 1))
                    last.then_inc(sem["qk"], 1)
                    if t >= 2:
                        after(pe, "v_out", t - 1)
                    for c in range(CT):
                        last = pe.matmul(PS[:, 4 + t % 2, 0:C], xT_next[:, c, t * P:(t + 1) * P], wqkvT[:, c, 2 * C:3 * C],
                                         start=(c == 0), stop=(c == CT - 1))
                    last.then_inc(sem["v"], 1)
                after(pe, "nlow", 1)
                pe.transpose(PS[0:1, 6, 0:P], norm_low[:, :], ident[:, :]).then_inc(sem["nlowT"], 1)

            def front_turn_q(f):
                g, half = f // 2, f % 2
                if f == 0:
                    after(pe, "qk_out", T)
                    after(pe, "scaled", 1)
                    after(pe, "flag", 1)
                if f >= 2:
                    after(pe, "q_ready", f - 1)
                for i in range(T // 2):
                    last = pe.transpose(PS[:, 6 + f % 2, i * P:(i + 1) * P],
                                        feat[:, 0, g, half * T // 2 + i].rearrange("p j s -> p (j s)"), ident[:, :])
                last.then_inc(sem["trq"], 1)

            def front_gmat(g):
                if g == 0:
                    after(pe, "v_out", T)
                    after(pe, "scaled", 2)
                after(pe, "q_ready", 2 * G - 1 + g % 2) if g < 2 else after(pe, "g_ready", g - 1)
                for t in range(T):
                    last = pe.matmul(PS[:, 6 + g % 2, 0:P],
                                     feat[:, 1, g, t].rearrange("p j s -> p (j s)"),
                                     v_aug[:, t, 4 * g:4 * g + 4, :].rearrange("p h s -> p (h s)"),
                                     start=(t == 0), stop=(t == T - 1))
                last.then_inc(sem["gmat"], 1)

            def turn_operand(g, e, general=False):
                split, turned, ready, n = ("split", "tr6", "op_ready", g - 1) if g else ("f_split", "f_tr6", "f_op_ready", 0)
                if e == 0:
                    after(pe, split, 4 * n + 4)
                if n or e:
                    after(pe, ready, 8 * n + e)
                if g == 0 and e == 0:
                    after(pe, "g_ready", G)
                if n and e == 0 and not general:
                    after(pe, "rden", 4 * n)
                for t in range(T):
                    last = pe.transpose(PS[0:KR, 7, :].bitcast(BF16)[:, t * P:(t + 1) * P],
                                        parts[:, e // 4, 4 * t + e % 4].rearrange("p s f -> p (s f)"), ident16[:, :])
                last.then_inc(sem[turned], 1)

            def batch(b, nxt):
                def scores(q):
                    g, qh, kt = q // (QH * T), q // T % QH, q % T
                    if q >= 2:
                        after(pe, "squared", q - 1)
                    if g and q % (QH * T) == 0:
                        after(pe, "op_ready", 8 * g)
                    for j in range(4):
                        if j == 2 and q >= 1:
                            after(pe, "z_out", q)
                        bank = 2 * (q % 2) + j if j < 2 else 2 + j
                        mm = pe.matmul(PS[:, bank, :], opT[g % 2][0:KR, 1, j, kt * P:(kt + 1) * P],
                                       opT[g % 2][0:KR, 0, j, qh * QW:(qh + 1) * QW], start=True, stop=True)
                        if j % 2:
                            mm.then_inc(sem["sc_act" if j == 1 else "sc_dve"], 1)

                def weigh(q):
                    g, qh, kt = q // (QH * T), q // T % QH, q % T
                    i = q // T
                    acc = PS[:, 6, :]
                    if kt == 0:
                        if i >= 1:
                            after(pe, "acc_out", i)
                        pe.matmul(acc, Gm[:, g, :], qT[:, g, qh * QW:(qh + 1) * QW], start=True, stop=False,
                                  skip_group_check=True)
                    after(pe, "rooted", q + 1)
                    for j in range(4):
                        mm = pe.matmul(acc[j * S:(j + 1) * S, :], v_aug[:, kt, 4 * g + j, :],
                                       root[:, q % NBUF, j * QW:(j + 1) * QW], start=False, stop=(kt == T - 1),
                                       skip_group_check=True)
                    mm.then_inc(sem["pv"], 1)

                def denominators(i):
                    g, qh = i // QH, i % QH
                    after(pe, "acc_out", i + 1)
                    if i:
                        after(pe, "rden", 2 * i)
                    after(pe, "op_ready", 8 * min(G - 1, i // QH + 1))
                    pe.matmul(PS[:, 7, :], den_pick[:, :], oT[:, g, qh * QW:(qh + 1) * QW],
                              start=True, stop=True).then_inc(sem["den"], 1)

                def general_products(g):
                    def body(qh, kt, j):
                        take(pe, "start")
                        pe.matmul(PS[:, 0, :], opT[g % 2][0:KR, 1, j, bass.ds(kt * P, P)],
                                  opT[g % 2][0:KR, 0, j, bass.ds(qh * QW, QW)], start=True, stop=True)
                        pe.matmul(PS[:, 1, :], one_minus_q[:, j, :], qT[:, g, bass.ds(qh * QW, QW)],
                                  start=True, stop=True).then_inc(hand["products"], 1)
                        take(pe, "weights")
                        pe.matmul(PS[j * S:(j + 1) * S, 6, :], g_v, g_weight, start=True, stop=True
                                  ).then_inc(hand["sums"], 1)
                    return body

                fast = load_flag(pe)
                with pe.If(fast == 1):
                    for q in range(QUADS + 2):
                        if q < QUADS:
                            scores(q)
                        if q >= 2:
                            weigh(q - 2)
                        at, gq = q % (QH * T), q // (QH * T)
                        if 0 < gq < G and at in (0, 3):
                            denominators(gq * QH - 2 + (at == 3))
                        if gq + 1 < G and at >= 8:
                            turn_operand(gq + 1, at - 8)
                    denominators(G * QH - 2)
                    denominators(G * QH - 1)

                    after(pe, "squared", QUADS)
                    after(pe, "z_out", QUADS)
                with pe.Else():
                    for g in range(G):
                        if g:
                            for e in range(8):
                                turn_operand(g, e, general=True)
                            after(pe, "op_ready", 8 * g)
                        every_key_tile(pe, general_products(g))
                    take(pe, "start")
                    for i in range(G * QH):
                        denominators(i)

                after(pe, "o_ready", G * QH)
                for t in range(T):
                    if t >= 2:
                        after(pe, "o_res", t - 1)
                    for g in range(G):
                        last = pe.matmul(PS[:, 4 + t % 2, 0:C], oT[:, g, t * P:(t + 1) * P], woT[:, g, :],
                                         start=(g == 0), stop=(g == G - 1))
                    last.then_inc(sem["oproj"], 1)
                for t in range(T):
                    transpose_x(0, t)
                after(pe, "xt", T)

                def x_scores(t):
                    if t >= 1:
                        after(pe, "shifted", t)
                    for i in range(4):
                        for c in range(CT):
                            last = pe.matmul(PS[:, i, 0:4 * NK], xT[:, c, t * P:(t + 1) * P],
                                             Mb[:, c, 4 * i * NK:4 * (i + 1) * NK],
                                             start=(c == 0), stop=(c == CT - 1))
                    last.then_inc(sem["xsc"], 1)

                def x_turn(t):
                    after(pe, "xnorm", t + 1)
                    for i in range(3):
                        if 3 * t + i >= 2:
                            after(pe, "pt_out", 3 * t + i - 1)
                        for k in range(4 * i, min(4 * i + 4, PT)):
                            n = P if k < PT - 1 else LAST
                            last = pe.transpose(PS[0:n, 4 + (3 * t + i) % 2, (k % 4) * P:(k % 4 + 1) * P],
                                                prob[:, t % 3, k * P:k * P + n], ident[:, :])
                        last.then_inc(sem["ptr"], 1)

                def x_weigh(t):
                    if t == 0:
                        after(pe, "mn_in", 48)
                    after(pe, "pt_out", 3 * t + 3)
                    if t >= 2:
                        after(pe, "x_res", t - 1)
                    for k in range(PT):
                        n = P if k < PT - 1 else LAST
                        last = pe.matmul(PS[:, 6 + t % 2, 0:C], pT[0:n, t % 2, k, :], Nb[0:n, k, :],
                                         start=(k == 0), stop=(k == PT - 1))
                    last.then_inc(sem["xo"], 1)

                after(pe, "o_res", T)
                after(pe, "mn_in", 48)
                after(pe, "o_ready", G * QH)
                for t in range(T + 2):
                    if t < T:
                        x_scores(t)
                    if 1 <= t <= T:
                        x_turn(t - 1)
                    if t >= 2:
                        x_weigh(t - 2)
                after(pe, "shifted", T)
                if nxt is not None:
                    front_transposes()
                    after(pe, "f_xt", T)
                for t in range(T):
                    transpose_x(1, t)
                after(pe, "xs", 1)
                for c in range(CT):
                    last = pe.matmul(PS[0:1, 7, 0:E], xsum[:, c:c + 1], Wr_sb[:, c, :],
                                     start=(c == 0), stop=(c == CT - 1))
                last.then_inc(sem["rsc"], 1)
                after(pe, "pt_out", 3 * T)
                if nxt is not None:
                    front_project()
                    after(pe, "flag", 1)
                after(pe, "xt", 2 * T)
                after(pe, "w1_in", PER["w1_in"])
                pe.transpose(PS[:, 6, 0:FT], b1_rows[:, :], ident[0:FT, 0:FT]).then_inc(sem["b1_tr"], 1)
                if nxt is not None:
                    after(pe, "qk_out", T)
                    after(pe, "b1_out", 1)
                for f in range(2 * FT):
                    ft, half = f // 2, f % 2
                    if f >= 4:
                        after(pe, "h_out", f - 3)
                    for c in range(CT):
                        last = pe.matmul(PS[:, f % 4, :], W1_sb[:, c, ft * P:(ft + 1) * P],
                                         xT[:, c, half * 512:(half + 1) * 512], start=(c == 0), stop=(c == CT - 1))
                    last.then_inc(sem["h_prod"], 1)
                    if nxt is not None:
                        for kind, i in SIDE.get(f, ()):
                            front_turn_q(i) if kind == "qT" else front_gmat(i)
                if nxt is not None:
                    after(pe, "v_out", T)
                after(pe, "w2_in", PER["w2_in"])
                after(pe, "h_out", 2 * FT)
                for t in range(T):
                    if nxt is not None:
                        turn_operand(0, t)
                    if t >= 2:
                        after(pe, "y_res", t - 1)
                    for f in range(FT):
                        last = pe.matmul(PS[:, 4 + t % 2, 0:C], hT[:, f, t * P:(t + 1) * P], W2_sb[:, f, :],
                                         start=(f == 0), stop=(f == FT - 1))
                    last.then_inc(sem["y"], 1)
                batch_end(pe)

            front_transposes()
            front_project()
            for f in range(2 * G):
                front_turn_q(f)
            for g in range(G):
                front_gmat(g)
            for e in range(8):
                turn_operand(0, e)
            batch_end(pe)
            all_batches(pe, batch)


_INS = ['x', 'ctx_768', 'L0_attn_wq', 'L0_attn_wk', 'L0_attn_wv', 'L0_attn_wo', 'L0_xattn_Wq', 'L0_xattn_Wk',
        'L0_xattn_Wv', 'L0_xattn_Wo', 'L0_xattn_bo', 'L0_ffn_Wr', 'L0_ffn_br', 'L0_ffn_W1', 'L0_ffn_b1',
        'L0_ffn_W2', 'L0_ffn_b2']
_OUTS = [((4, 1024, 256), 'float32')]


def kernel(**inputs):
    import numpy as _np
    import concourse.bacc as _bacc
    from concourse import mybir as _mybir
    from concourse.bass_utils import run_bass_kernel_spmd as _run

    nc = _bacc.Bacc("TRN2", target_bir_lowering=False, num_devices=1)
    arrays, args = {}, []
    for name in _INS:
        a = _np.ascontiguousarray(inputs[name])
        arrays[f"in_{name}_dram"] = a
        args.append(nc.dram_tensor(f"in_{name}_dram", a.shape, _mybir.dt.from_np(a.dtype), kind="ExternalInput").ap())
    for i, (shape, dtype) in enumerate(_OUTS):
        dt = _mybir.dt.from_np(_np.dtype(dtype))
        args.append(nc.dram_tensor(f"out_{i}_dram", shape, dt, kind="ExternalOutput").ap())
    decoder_layer(nc, *args)
    r = _run(nc, [arrays], core_ids=[0])
    return r.results[0]["out_0_dram"]
```

```python
from contextlib import ExitStack

import concourse.bass as bass
from concourse import mybir

F32 = mybir.dt.float32
BF16 = mybir.dt.bfloat16
I32 = mybir.dt.int32
U32 = mybir.dt.uint32
ALU = mybir.AluOpType
ACT = mybir.ActivationFunctionType
AX = mybir.AxisListType.X

P = 128
EPS = 1e-5
NORM_MIN = 96.0
DENOM_MIN = 1e-6


def decoder_layer(nc, x, ctx_in, wq, wk, wv, wo, Wq, Wk, Wv, Wo, bo, Wr, br, W1, b1, W2, b2, out):
    B, N, C = x.shape
    H = 16
    D = C // H
    S = 32
    NK, CE = ctx_in.shape[1:]
    CEH = CE // 2
    INNER = Wq.shape[1]
    E, _, FF = W1.shape
    T = N // P
    CT = C // P
    G = H // 4
    QW = 512
    QH = N // QW
    QUADS = G * QH * T
    HP = H // 2
    FT = FF // P
    NKEY = H * NK
    PT = -(-NKEY // P)
    LAST = NKEY - (PT - 1) * P

    ctx = ExitStack()
    with ctx:
        def sb(name, shape, dt=F32):
            return ctx.enter_context(nc.sbuf_tensor(name, shape, dt))

        ident = sb("ident", [P, P])
        ident16 = sb("ident16", [P, P], BF16)
        wqkvT = sb("wqkvT", [P, CT, 3 * C])
        woT = sb("woT", [P, G, C])
        Wr_sb = sb("Wr_sb", [P, CT, E])
        br_sb = sb("br_sb", [1, E])
        bo_sb = sb("bo_sb", [P, C])
        neg_block = sb("neg_block", [P, P])
        den_pick = sb("den_pick", [P, P])
        x_raw = sb("x_raw", [P, T, C])
        x_res = sb("x_res", [P, T, C])
        xT = sb("xT", [P, CT, N])
        arena_a = sb("arena_a", [P, T * 2 * H * S])
        feat = arena_a[:, :].rearrange("p (w g t j s) -> p w g t j s", w=2, g=G, t=T, j=4)
        m_w = CT * NKEY
        Mb = arena_a[:, 0:m_w].rearrange("p (c k) -> p c k", c=CT)
        Nb = arena_a[:, m_w:m_w + PT * C].rearrange("p (i o) -> p i o", i=PT)
        pT = arena_a[:, m_w + PT * C:m_w + PT * C + 2 * PT * P].rearrange("p (b i q) -> p b i q", b=2, i=PT)
        v_aug = sb("v_aug", [P, T, H, S])
        NF, NS = D + 2, 6
        KR = NS * NF
        arena_b = sb("arena_b", [P, 2 * G * N])
        arena_s = sb("arena_s", [P, 7680])
        g_sums = arena_b[:, 0:G * N].rearrange("p (g n) -> p g n", g=G)
        opT = (arena_s[:, 0:G * N].bitcast(BF16).rearrange("p (w j n) -> p w j n", w=2, j=4),
               arena_b[:, G * N:2 * G * N].bitcast(BF16).rearrange("p (w j n) -> p w j n", w=2, j=4))
        n_parts = 2 * T * 4 * KR // 2
        parts = arena_s[:, G * N:G * N + n_parts].bitcast(BF16).rearrange(
            "p (w x s f) -> p w x s f", w=2, x=T * 4, s=NS)
        rest = sb("rest", [P, 2, T * 4, NF])
        hT = arena_b[:, :].rearrange("p (f n) -> p f n", f=FT)
        oT = sb("oT", [P, G, N])
        qT = oT
        NBUF = 4
        LAG = 3
        SPARE = (1, 9, 13)
        arena_t = sb("arena_t", [P, NBUF * 4 * QW])
        x_hat = arena_t[:, NBUF * 4 * QW - T * C:].rearrange("p (t c) -> p t c", t=T)
        root = arena_t[:, :].rearrange("p (b j q) -> p b (j q)", b=NBUF, j=4)
        xT_next = arena_t[:, CT * FF + FT * C:CT * FF + FT * C + CT * N].rearrange("p (c n) -> p c n", c=CT)
        sq = arena_s[:, G * N:G * N + 2 * 2 * C].rearrange("p (b c) -> p b c", b=2)
        gen = arena_t[:, 0:6 * QW].rearrange("p (i q) -> p i q", i=6)
        g_denom, g_over, g_u, g_root, g_root2, g_weight = (gen[:, i, :] for i in range(6))
        one_minus_q = arena_t[:, 6 * QW:7 * QW].rearrange("p (j m) -> p j m", j=4)
        g_v = arena_t[:, 7 * QW:7 * QW + S]
        g_k = arena_t[:, 7 * QW + S:7 * QW + S + 1]
        Wq_nat = arena_a[:, 0:CT * INNER].rearrange("p (c i) -> p c i", c=CT)
        Wk_sb = arena_a[0:CEH, 2048:4096].rearrange("p (c i) -> p c i", c=2)
        Wv_sb = arena_a[0:CEH, 4096:6144].rearrange("p (c i) -> p c i", c=2)
        Wo_sb = arena_a[:, 6144:8192].rearrange("p (h o) -> p h o", h=HP)
        w_nat = arena_b[:, 0:3 * CT * C].rearrange("p (w c i) -> p w c i", w=3, c=CT)
        wo_pad = arena_b[:, 2048:2048 + CT * G * P].rearrange("p (c g j s) -> p c g j s", c=CT, g=G, j=4)
        WqT = arena_b[:, 4096:4096 + HP * C].rearrange("p (h c) -> p h c", h=HP)
        ctxT = arena_b[0:CEH, 6144:6144 + 2 * B * NK].rearrange("p (c b k) -> p c b k", c=2, b=B)
        ctx_sb = arena_b[0:NK, 3072:3072 + B * CE].rearrange("p (b c) -> p b c", b=B)
        kx = arena_t[:, 0:HP * B * NK].rearrange("p (h b k) -> p h b k", h=HP, b=B)
        vx = arena_t[:, HP * B * NK:2 * HP * B * NK].rearrange("p (h b k) -> p h b k", h=HP, b=B)
        prob = arena_t[:, 0:3 * NKEY].rearrange("p (b k) -> p b k", b=3)
        W1_sb = arena_t[:, 0:CT * FF].rearrange("p (c f) -> p c f", c=CT)
        W2_sb = arena_t[:, CT * FF:CT * FF + FT * C].rearrange("p (f o) -> p f o", f=FT)
        Gm = sb("Gm", [P, G, P])
        norms = sb("norms", [P, 2, G, T, 4])
        one_minus = sb("one_minus", [P, 2, G, T, 4])
        inv = sb("inv", [P, 2, G, T, 4])
        recip_den = sb("recip_den", [P, QW // P, 4])
        den_rows = arena_b[:, 0:QW].rearrange("p (t j s) -> p t j s", j=4, s=S)
        stats, meanvar, std, rstd = (sb(n, [P, 2, T, w]) for n, w in (("stats", 6), ("meanvar", 2), ("std", 1), ("rstd", 1)))
        norm_low = sb("norm_low", [P, 1])
        low1 = sb("low1", [1, 1])
        fast_flag = sb("fast_flag", [1, 1], I32)
        pmax = sb("pmax", [P, 2, H])
        psumr = sb("psumr", [P, 2, H])
        pinv = sb("pinv", [P, 2, H])
        xsum = sb("xsum", [P, 2, CT])
        route_s = sb("route_s", [1, E])
        route_m = sb("route_m", [1, 8])
        route_i = sb("route_i", [1, 8], U32)
        b1_rows = sb("b1_rows", [FT, P])
        b1_sb = sb("b1_sb", [P, FT])
        b2_sb = sb("b2_sb", [P, C])
        n_dram = nc.dram_tensor("n_rows_dram", (B, NKEY, C), F32, kind="Internal").ap()
        m_dram = nc.dram_tensor("m_cols_dram", (B, C, NKEY), F32, kind="Internal").ap()
        n_stage = [oT[0:NK, :, :].rearrange("p g n -> p (g n)").rearrange("p (h o) -> p h o", h=H),
                   arena_s[0:NK, 0:H * C].rearrange("p (h o) -> p h o", h=H)]
        m_stage = arena_s[:, 0:B * NKEY].rearrange("p (b h k) -> p b h k", b=B, h=H)
        SETS = (("m", 0, 1), ("n", 0, 0), ("m", 1, 1), ("n", 1, 0), ("n", 2, 1), ("n", 3, 0))

        def stored_before(n, st):
            return sum(which == st for _, _, which in SETS[:n])

        PS = ctx.enter_context(nc.psum_tensor("PS", [P, 8, 512], F32))

        LAST_SUMS = G * QH - 1
        TH = T // 2

        def den_bank(i):
            return 4 if i == LAST_SUMS else 7

        def o_bank(t):
            return PS[:, 7 if t < TH or t % 2 else 5, 0:C]

        def tr_bank(i, t):
            return PS[:, t % 2 + (6 if i == 0 and t >= TH else 0), 0:C]

        def squared_by_scalar(q):
            return 1 if q % (QH * T) in SPARE else 2

        def squared_by_vector(q):
            return sum(squared_by_scalar(i) == 1 for i in range(q + 1))

        PER = dict(
            x_in=16, presets=4, f_stats=1, f_std=1, f_xhat=T, f_tr=T, f_xt=T,
            qk=T, v=T, squares=T, qk_out=T, norm=T, v_out=T,
            nlow=1, nlowT=1, flag=1, scaled=2,
            trq=2 * G, q_ready=2 * G, gmat=G, g_ready=G, f_split=4, f_tr6=8, f_op_ready=8,
            split=4 * (G - 1), tr6=8 * (G - 1), op_ready=8 * (G - 1),
            sc_act=QUADS, sc_dve=QUADS, squared=QUADS, z_out=QUADS, z_sq=QUADS, z_sq_dve=squared_by_vector(QUADS - 1), rooted=QUADS, pv=QUADS,
            acc_out=G * QH, den=G * QH, inverse=G * QH, rden=G * QH, spread=G * QH, o_ready=LAST_SUMS + 4,
            x_res_free=1, oproj=T, o_res=T,
            stats=3, std=3, xhat=2 * T, tr=2 * T, xt=2 * T,
            mn_in=48, bo_added=1,
            xsc=T, xmax=T, shifted=T, xexp=T, xsum=T, xinv=T, xnorm=T, ptr=3 * T, pt_out=3 * T, xo=T, x_res=T,
            xs=2, rsc=1, route=1, w1_in=32, w2_in=32, b1_tr=1, b1_out=1, b2_added=1,
            h_prod=2 * FT, h_out=2 * FT, y=T, y_res=T,
            dve_step=100,
            batch_done=4,
        )
        sem = {k: ctx.enter_context(nc.semaphore("s_" + k)) for k in PER}
        once = {k: ctx.enter_context(nc.semaphore("s_" + k)) for k in
                ("kv_weights", "weights", "setup", "ctx_tr", "ctx_out", "wtr", "wtr_out", "kvx", "kvx_out", "mn", "m_out", "n_out", "stored0", "stored1")}
        SETUP_STEPS = 13
        go, gone, stored = (ctx.enter_context(nc.semaphore("s_" + k)) for k in ("go", "gone", "stored"))
        hand = {k: ctx.enter_context(nc.semaphore("s_gen_" + k)) for k in
                ("start", "products", "u", "roots", "weights", "sums")}
        first, last_sem = sem["x_in"].num, sem["batch_done"].num
        assert last_sem - first == len(sem) - 1

        def after(eng, name, n):
            assert 0 < n <= PER[name]
            eng.wait_ge(sem[name], n)

        def all_batches(eng, batch):
            with eng.Fori(0, B - 1) as b:
                batch(b, b + 1)
            batch(B - 1, None)

        def batch_end(eng):
            eng.drain().then_inc(sem["batch_done"], 1)
            eng.wait_ge(go, 1)
            eng.sem_inc(gone, 1)

        def take(eng, name):
            eng.wait_ge(hand[name], 1)
            eng.sem_clear(hand[name])

        def every_key_tile(eng, body):
            with eng.Fori(0, QH) as qh:
                with eng.Fori(0, T) as kt:
                    for j in range(4):
                        body(qh, kt, j)

        def load_flag(eng):
            return eng.value_load(fast_flag[0:1, 0:1], min_val=0, max_val=1)

        SIDE = {f: [("qT", 2 * f - 12), ("qT", 2 * f - 11)] for f in range(6, 10)}
        SIDE[0] = [("low", 0)]
        SIDE.update({f: [("Gm", f - 10)] for f in range(10, 14)})

        N_WEIGHT_DMAS = 1 + 3 + CT * G + 1 + 3

        block = ctx.enter_context(nc.Block())

        @block.sync
        def _(sp):
            def load_x(b):
                sp.dma_start(x_raw[:, :, :], x[bass.ds(b, 1)].rearrange("a (t p) c -> p (a t) c", p=P)
                             ).then_inc(sem["x_in"], 16)

            sp.dma_start(ctx_sb, ctx_in.rearrange("b k c -> k b c")).then_inc(once["kv_weights"], 16)
            for dst, w in ((Wk_sb, Wk), (Wv_sb, Wv)):
                sp.dma_start(dst, w.rearrange("(c p) i -> p c i", p=CEH)).then_inc(once["kv_weights"], 16)
            sp.dma_start(Wq_nat, Wq.rearrange("(c p) i -> p c i", p=P)).then_inc(once["weights"], 16)
            for i, w in enumerate((wq, wk, wv)):
                sp.dma_start(w_nat[:, i], w.rearrange("(c p) i -> p c i", p=P)).then_inc(once["weights"], 16)
            sp.wait_ge(once["setup"], 1)
            for c in range(CT):
                for g in range(G):
                    sp.dma_start(wo_pad[:, c, g, :, 0:D], wo[c * P:(c + 1) * P, g * 4 * D:(g + 1) * 4 * D]
                                 .rearrange("p (j d) -> p j d", j=4)).then_inc(once["weights"], 16)
            sp.dma_start(Wo_sb, Wo.rearrange("(h p) o -> p h o", p=P)).then_inc(once["weights"], 16)
            sp.dma_start(Wr_sb[:, :, :], Wr.rearrange("(c p) e -> p c e", p=P)).then_inc(once["weights"], 16)
            sp.dma_start(br_sb[:, :], br.rearrange("(a e) -> a e", a=1)).then_inc(once["weights"], 16)
            sp.dma_start(bo_sb[:, :], bo.rearrange("(a c) -> a c", a=1).to_broadcast([P, C])).then_inc(once["weights"], 16)
            load_x(0)
            done_n, done_m = 0, 0
            for kind, i, st in SETS:
                if kind == "n":
                    done_n += H // 2
                    sp.wait_ge(once["n_out"], done_n)
                    sp.dma_start(n_dram[i].rearrange("(h k) o -> k h o", h=H), n_stage[st]).then_inc(once[f"stored{st}"], 16)
                else:
                    done_m += H
                    sp.wait_ge(once["m_out"], done_m)
                    sp.dma_start(m_dram[:, i * P:(i + 1) * P, :].rearrange("b p k -> p b k"),
                                 m_stage.rearrange("p b h k -> p b (h k)")).then_inc(once["stored1"], 16)
            for st in range(2):
                sp.wait_ge(once[f"stored{st}"], 16 * stored_before(len(SETS), st))
            def all_meet():
                after(sp, "batch_done", 4)
                sp.sem_clear(range(first, last_sem + 1))
                sp.sem_inc(go, 1)
                sp.wait_ge(gone, 4)
                sp.sem_clear(go)
                sp.sem_clear(gone)

            def batch(b, nxt):
                sp.wait_ge(stored, 32)
                sp.sem_clear(stored)
                sp.sem_inc(sem["x_res_free"], 1)
                after(sp, "split", PER["split"])
                sp.dma_start(Mb, m_dram[bass.ds(b, 1)].rearrange("a (c p) k -> p (a c) k", p=P)).then_inc(sem["mn_in"], 16)
                sp.dma_start(Nb[:, 0:PT - 1, :], n_dram[bass.ds(b, 1), 0:(PT - 1) * P, :]
                             .rearrange("a (i p) o -> p (a i) o", p=P)).then_inc(sem["mn_in"], 16)
                sp.dma_start(Nb[0:LAST, PT - 1, :], n_dram[bass.ds(b, 1), (PT - 1) * P:NKEY, :]
                             .rearrange("a p o -> (a p) o")).then_inc(sem["mn_in"], 16)
                if nxt is not None:
                    after(sp, "o_res", T)
                    load_x(nxt)
                after(sp, "route", 1)
                e = sp.value_load(route_i[0:1, 0:1], min_val=0, max_val=E - 1)
                sp.dma_start(W1_sb, W1[bass.ds(e, 1)].rearrange("a (c p) f -> p (a c) f", p=P)).then_inc(sem["w1_in"], 16)
                sp.dma_start(b1_rows[:, :], b1[bass.ds(e, 1)].rearrange("a (f p) -> (a f) p", p=P)).then_inc(sem["w1_in"], 16)
                sp.dma_start(b2_sb[:, :], b2[bass.ds(e, 1)].to_broadcast([P, C])).then_inc(sem["w2_in"], 16)
                sp.dma_start(W2_sb, W2[bass.ds(e, 1)].rearrange("a (f p) o -> p (a f) o", p=P)).then_inc(sem["w2_in"], 16)
                for half in range(2):
                    t0 = half * T // 2
                    after(sp, "y_res", t0 + T // 2)
                    sp.dma_start(out[bass.ds(b, 1)].rearrange("a (t p) c -> p (a t) c", p=P)[:, t0:t0 + T // 2],
                                 x_res[:, t0:t0 + T // 2, :]).then_inc(stored, 16)
                all_meet()

            all_meet()
            sp.sem_inc(stored, 32)
            all_batches(sp, batch)
            sp.wait_ge(stored, 32)

        @block.gpsimd
        def _(pool):
            done = [0]

            def setup(ins):
                done[0] += 1
                ins.then_inc(once["setup"], 1)
                pool.wait_ge(once["setup"], done[0])

            setup(pool.memset(wo_pad, 0.0))
            setup(pool.memset(ident[:, :], 0.0))
            setup(pool.affine_select(out=ident[:, :], in_=ident[:, :], compare_op=ALU.not_equal, fill=1.0,
                                     base=0, pattern=[[-1, P]], channel_multiplier=1))
            setup(pool.tensor_copy(ident16[:, :], ident[:, :]))
            setup(pool.memset(den_pick[:, :], 0.0))
            pick = den_pick[:, :].rearrange("p (j m) -> p j m", j=4)
            setup(pool.affine_select(out=pick, in_=pick, compare_op=ALU.not_equal, fill=1.0, base=-D,
                                     pattern=[[-S, 4], [0, S]], channel_multiplier=1))
            setup(pool.memset(neg_block[:, :], 0.0))
            for j in range(4):
                setup(pool.memset(neg_block[j * S:(j + 1) * S, j * S:(j + 1) * S], -1.0))
            setup(pool.memset(v_aug[:, :, :, D:S].rearrange("p t h s -> p (t h) s"), 0.0))
            setup(pool.memset(v_aug[:, :, :, D:D + 1].rearrange("p t h s -> p (t h) s"), 1.0))
            assert done[0] == SETUP_STEPS
            pool.wait_ge(once["m_out"], 2 * H)
            pool.wait_ge(once["n_out"], B * H // 2)
            def front():
                flat = feat.rearrange("p w g t j s -> p (w g t j) s")
                half = flat.shape[1] // 2
                presets = ((flat[:, :, D + 3:S], 0.0), (flat[:, :, D + 2:D + 3], 1.0),
                           (flat[:, 0:half, D + 1:D + 2], 1.0), (flat[:, half:2 * half, D:D + 1], 2.0))
                for i, (places, value) in enumerate(presets):
                    pool.memset(places, value).then_inc(sem["presets"], 1)
                    after(pool, "presets", i + 1)

            def batch(b, nxt):
                fast = load_flag(pool)
                with pool.If(fast == 1):
                    for q in range(QUADS):
                        after(pool, "z_out", q + 1)
                        zt = root[:, q % NBUF, 2 * QW:4 * QW]
                        pool.tensor_tensor(zt, zt, zt, ALU.mult).then_inc(sem["z_sq"], 1)
                after(pool, "xhat", T)
                pool.tensor_tensor(x_res[:, :, :], x_res[:, :, :],
                                   bo_sb[:, None, :].to_broadcast([P, T, C]), ALU.add).then_inc(sem["bo_added"], 1)
                if nxt is not None:
                    after(pool, "xo", T)
                    front()
                after(pool, "xhat", 2 * T)
                after(pool, "w2_in", PER["w2_in"])
                pool.tensor_tensor(x_res[:, :, :], x_res[:, :, :],
                                   b2_sb[:, None, :].to_broadcast([P, T, C]), ALU.add).then_inc(sem["b2_added"], 1)
                batch_end(pool)

            front()
            batch_end(pool)
            all_batches(pool, batch)

        @block.scalar
        def _(act):
            def front_std():
                after(act, "f_stats", 1)
                act.activation(std[:, 1, :, 0], meanvar[:, 1, :, 1], ACT.Sqrt, bias=EPS).then_inc(sem["f_std"], 1)

            for c in range(2):
                act.wait_ge(once["ctx_tr"], 1 + c)
                act.activation(ctxT[:, c], PS[0:CEH, 4 + c, 0:B * NK].rearrange("p (b k) -> p b k", b=B), ACT.Copy
                               ).then_inc(once["ctx_out"], 1)
            for i in range(2 * HP):
                act.wait_ge(once["kvx"], i + 1)
                act.activation((kx, vx)[i // HP][:, i % HP], PS[:, i % 4, 0:B * NK].rearrange("p (b k) -> p b k", b=B),
                               ACT.Copy).then_inc(once["kvx_out"], 1)
            turned = ([(WqT[:, 2 * i:2 * i + 2, :], 4 + i) for i in range(4)]
                      + [(wqkvT[:, :, i * C:(i + 1) * C], i) for i in range(3)]
                      + [(woT[:, 2 * i:2 * i + 2, :], 3 + i) for i in range(2)])
            for n, (places, bank) in enumerate(turned):
                act.wait_ge(once["wtr"], n + 1)
                act.activation(places, PS[:, bank, :].rearrange("p (c o) -> p c o", c=2), ACT.Copy
                               ).then_inc(once["wtr_out"], 1)
            front_std()
            at, stored = 0, 0
            for n, (kind, i, st) in enumerate(SETS):
                if kind == "m":
                    at += H
                    continue
                if stored_before(n, st):
                    act.wait_ge(once[f"stored{st}"], 16 * stored_before(n, st))
                for k in range(H // 2):
                    at += 1
                    act.wait_ge(once["mn"], at)
                    heads = 4 * (k // 2) + k % 2
                    act.activation(n_stage[st][:, heads:heads + 3:2, :],
                                   PS[0:NK, 4 + k % 4, :].rearrange("p (h o) -> p h o", h=2), ACT.Copy
                                   ).then_inc(once["n_out"], 1)

            def layer_norm_std(i, tiles):
                after(act, "stats", i + 1)
                act.activation(std[:, 0, tiles, 0], meanvar[:, 0, tiles, 1], ACT.Sqrt, bias=EPS).then_inc(sem["std"], 1)

            def xT_out(i, t):
                after(act, "tr", i * T + t + 1)
                act.activation(xT[:, :, t * P:(t + 1) * P], tr_bank(i, t).rearrange("p (c n) -> p c n", c=CT),
                               ACT.Copy).then_inc(sem["xt"], 1)

            def front_transposed():
                for t in range(T):
                    after(act, "f_tr", t + 1)
                    act.activation(xT_next[:, :, t * P:(t + 1) * P], PS[:, t % 4, 0:C].rearrange("p (c n) -> p c n", c=CT),
                                   ACT.Copy).then_inc(sem["f_xt"], 1)

            def front_projected(tiles=range(T)):
                for t in tiles:
                    after(act, "qk", t + 1)
                    if t >= 2:
                        after(act, "norm", t - 1)
                    src = PS[:, 2 + t % 2, :]
                    act.activation(sq[:, t % 2, :], src, ACT.Square).then_inc(sem["squares"], 1)
                    if t == 0:
                        after(act, "presets", 4)
                    act.activation(feat[:, 0, :, t, :, 0:D], src[:, 0:C].rearrange("p (g j d) -> p g j d", g=G, j=4), ACT.Copy)
                    act.activation(feat[:, 1, :, t, :, 0:D], src[:, C:2 * C].rearrange("p (g j d) -> p g j d", g=G, j=4),
                                   ACT.Copy, scale=-4.0).then_inc(sem["qk_out"], 1)

            def front_qT(f):
                g, half = f // 2, f % 2
                after(act, "trq", f + 1)
                act.activation(qT[:, g, half * 512:(half + 1) * 512], PS[:, 6 + f % 2, :], ACT.Copy
                               ).then_inc(sem["q_ready"], 1)

            def batch(b, nxt):
                def square(q):
                    after(act, "sc_act", q + 1)
                    if q >= NBUF:
                        after(act, "pv", q - NBUF + 1)
                    n = squared_by_scalar(q)
                    act.activation(root[:, q % NBUF, 0:n * QW],
                                   PS[:, 2 * (q % 2):2 * (q % 2) + n, :].rearrange("p j q -> p (j q)"),
                                   ACT.Square, bias=1.0).then_inc(sem["squared"], 1)

                def take_root(q):
                    after(act, "squared", q + 1)
                    after(act, "z_sq", q + 1)
                    if squared_by_scalar(q) == 1:
                        after(act, "z_sq_dve", squared_by_vector(q))
                    act.activation(root[:, q % NBUF, :], root[:, q % NBUF, :], ACT.Sqrt, bias=-1.0
                                   ).then_inc(sem["rooted"], 1)

                def general_roots(qh, kt, j):
                    take(act, "u")
                    act.activation(g_root, g_u, ACT.Sqrt)
                    act.activation(g_root2, g_u, ACT.Sqrt, bias=2.0).then_inc(hand["roots"], 1)

                fast = load_flag(act)
                with act.If(fast == 1):
                    for q in range(QUADS):
                        square(q)
                        if q >= 1:
                            take_root(q - 1)
                    take_root(QUADS - 1)
                with act.Else():
                    for g in range(G):
                        every_key_tile(act, general_roots)

                for half in range(2):
                    layer_norm_std(half, slice(half * TH, (half + 1) * TH))
                    for t in range(half * TH, (half + 1) * TH):
                        xT_out(0, t)

                def p_out(t, i):
                    n = min(4, PT - 4 * i)
                    after(act, "ptr", 3 * t + i + 1)
                    act.activation(pT[:, t % 2, 4 * i:4 * i + n, :],
                                   PS[:, 4 + (3 * t + i) % 2, 0:n * P].rearrange("p (i q) -> p i q", i=n), ACT.Copy
                                   ).then_inc(sem["pt_out"], 1)

                for t in range(T + 1):
                    if t == T and nxt is not None:
                        front_std()
                    if t >= 1:
                        if t >= 3:
                            after(act, "xo", t - 2)
                        for i in range(3):
                            p_out(t - 1, i)
                    if t < T:
                        after(act, "shifted", t + 1)
                        act.activation(prob[:, t % 3, :], prob[:, t % 3, :], ACT.Exp).then_inc(sem["xexp"], 1)
                if nxt is not None:
                    front_transposed()
                layer_norm_std(2, slice(0, T))
                if nxt is not None:
                    front_projected(range(1))
                for t in range(T):
                    xT_out(1, t)
                if nxt is not None:
                    front_projected(range(1, T))
                after(act, "b1_tr", 1)
                act.activation(b1_sb[:, :], PS[:, 7, 0:FT], ACT.Copy).then_inc(sem["b1_out"], 1)
                after(act, "b1_out", 1)
                for f in range(2 * FT):
                    after(act, "h_prod", f + 1)
                    act.activation(hT[:, f // 2, (f % 2) * 512:(f % 2 + 1) * 512], PS[:, f % 4, :], ACT.Relu,
                                   bias=b1_sb[:, f // 2:f // 2 + 1]).then_inc(sem["h_out"], 1)
                    if nxt is not None:
                        for kind, i in SIDE.get(f, ()):
                            if kind == "qT":
                                front_qT(i)
                batch_end(act)

            front_transposed()
            for st in range(2):
                act.wait_ge(once[f"stored{st}"], 16 * stored_before(len(SETS), st))
            front_projected()
            for f in range(2 * G):
                front_qT(f)
            batch_end(act)
            all_batches(act, batch)

        @block.vector
        def _(dve):
            steps = [0]

            def step(ins):
                steps[0] += 1
                ins.then_inc(sem["dve_step"], 1)
                after(dve, "dve_step", steps[0])

            def tile_stats(src, t, of_next=0):
                return dve.bn_stats(stats[:, of_next, t, :], src[:, t, :])

            def layer_norm(src, names, i=0, of_next=0, x_hat_free=None, t0=0, t1=T):
                norm_aggregate(names[0], of_next, t0, t1)
                norm_apply(src, names[1:], i, of_next, x_hat_free, t0, t1)

            def norm_aggregate(at_stats, of_next, t0, t1):
                for t in range(t0, t1):
                    ins = dve.bn_aggr(meanvar[:, of_next, t, :], stats[:, of_next, t, :])
                ins.then_inc(sem[at_stats], 1)

            def norm_apply(src, names, i, of_next, x_hat_free, t0, t1):
                at_std, at_xhat = names
                mv, r_std = meanvar[:, of_next], rstd[:, of_next]
                after(dve, at_std, i + 1)
                step(dve.reciprocal(r_std[:, t0:t1, 0], std[:, of_next, t0:t1, 0]))
                if x_hat_free:
                    after(dve, *x_hat_free)
                for t in range(t0, t1):
                    dve.tensor_scalar(x_hat[:, t, :], src[:, t, :], mv[:, t, 0:1], r_std[:, t, :],
                                      ALU.subtract, ALU.mult).then_inc(sem[at_xhat], 1)

            def front_stats(tiles):
                after(dve, "x_in", 16)
                for t in tiles:
                    ins = tile_stats(x_raw, t, of_next=1)
                    if t == T - 1:
                        step(ins)

            def front_norm(x_hat_free=None):
                layer_norm(x_raw, ("f_stats", "f_std", "f_xhat"), of_next=1, x_hat_free=x_hat_free)

            norms_flat, om_flat, inv_flat = (a[:, :, :, :, :].rearrange("p w g t j -> p (w g t j)")
                                             for a in (norms, one_minus, inv))
            half_n = T * H
            flat = feat.rearrange("p w g t j s -> p (w g t j) s")

            def front_v_out(t):
                after(dve, "v", t + 1)
                dve.tensor_copy(v_aug[:, t, :, 0:D], PS[:, 4 + t % 2, 0:C].rearrange("p (h d) -> p h d", h=H)
                                ).then_inc(sem["v_out"], 1)

            def front_features(v_done=0):
                for t in range(T):
                    after(dve, "squares", t + 1)
                    dve.tensor_reduce(norms[:, :, :, t, :].rearrange("p w g j -> p (w g) j"),
                                      sq[:, t % 2, :].rearrange("p (h j d) -> p h j d", j=4, d=D), AX, ALU.add
                                      ).then_inc(sem["norm"], 1)
                    if t >= v_done:
                        front_v_out(t)
                after(dve, "norm", T)
                dve.tensor_reduce(norm_low[:, :], norms_flat, AX, ALU.min
                                  ).then_inc(sem["nlow"], 1)
                step(dve.tensor_scalar(om_flat, norms_flat, -1.0, 1.0, ALU.mult, ALU.add))
                step(dve.reciprocal(inv_flat, om_flat))
                after(dve, "presets", 4)
                dve.tensor_copy(flat[:, 0:half_n, D], norms_flat[:, 0:half_n])
                step(dve.tensor_scalar(flat[:, half_n:2 * half_n, D + 1], norms_flat[:, half_n:2 * half_n], 2.0, None, ALU.mult))
                after(dve, "nlowT", 1)
                step(dve.tensor_reduce(low1[:, :], PS[0:1, 6, 0:P], AX, ALU.min))
                dve.tensor_scalar(fast_flag[:, :], low1[:, :], NORM_MIN, None, ALU.is_ge).then_inc(sem["flag"], 1)
                after(dve, "flag", 1)
                with dve.If(load_flag(dve) == 0):
                    dve.memset(inv_flat, 1.0)
                    dve.drain()
                after(dve, "qk_out", T)
                for w in range(2):
                    part = flat[:, w * half_n:(w + 1) * half_n, 0:NF]
                    dve.tensor_tensor(part, part, inv_flat[:, w * half_n:(w + 1) * half_n, None]
                                      .to_broadcast([P, half_n, NF]), ALU.mult).then_inc(sem["scaled"], 1)
                after(dve, "scaled", 2)

            def group(g):
                return feat[:, :, g, :, :, 0:NF].rearrange("p w t j s -> p w (t j) s")

            def high_q(g):
                f = group(g)[:, 0]
                dve.tensor_copy(parts[:, 0, :, 0:4:3, :], f[:, :, None, :].to_broadcast([P, T * 4, 2, NF])
                                ).then_inc(sem["dve_step"], 1)
                dve.tensor_copy(parts[:, 0, :, 5, :], f).then_inc(sem["dve_step"], 1)
                steps[0] += 2

            def high_k(g):
                f = group(g)[:, 1]
                step(dve.tensor_copy(parts[:, 1, :, 0:3, :], f[:, :, None, :].to_broadcast([P, T * 4, 3, NF])))

            def less_high(g):
                step(dve.tensor_tensor(rest[:, :, :, :], group(g), parts[:, :, :, 0, :], ALU.subtract))

            def middle(g):
                name, base = ("split", 4 * (g - 1)) if g else ("f_split", 0)
                dve.tensor_copy(parts[:, 0, :, 1:5:3, :], rest[:, 0, :, None, :].to_broadcast([P, T * 4, 2, NF])
                                ).then_inc(sem[name], 1)
                dve.tensor_copy(parts[:, 1, :, 3:5, :], rest[:, 1, :, None, :].to_broadcast([P, T * 4, 2, NF])
                                ).then_inc(sem[name], 1)
                after(dve, name, base + 2)

            def low(g):
                for w, m, l in ((0, 1, 2), (1, 3, 5)):
                    dve.tensor_tensor(parts[:, w, :, l, :], rest[:, w], parts[:, w, :, m, :], ALU.subtract
                                      ).then_inc(sem["split" if g else "f_split"], 1)

            def operand_out(g, e):
                turned, ready, base = ("tr6", "op_ready", 8 * (g - 1)) if g else ("f_tr6", "f_op_ready", 0)
                after(dve, turned, base + e + 1)
                dve.tensor_copy(opT[g % 2][0:KR, e // 4, e % 4, :], PS[0:KR, 7, :].bitcast(BF16)
                                ).then_inc(sem[ready], 1)

            def front_parts():
                high_q(0)
                high_k(0)
                less_high(0)
                middle(0)
                low(0)
                for g in range(G):
                    after(dve, "gmat", g + 1)
                    dve.tensor_tensor(Gm[:, g, :], PS[:, 6 + g % 2, 0:P], neg_block[:, :], ALU.mult
                                      ).then_inc(sem["g_ready"], 1)

            def batch(b, nxt):
                steps[0] = 0

                def acc_out(i):
                    g, qh = i // QH, i % QH
                    after(dve, "pv", T * (i + 1))
                    dve.tensor_copy(oT[:, g, qh * QW:(qh + 1) * QW], PS[:, 6, :]).then_inc(sem["acc_out"], 1)

                def recip(i):
                    after(dve, "den", i + 1)
                    dve.reciprocal(recip_den[:, :, :], PS[:, den_bank(i), 0:QW // P * 4].rearrange("p (t j) -> p t j", j=4)
                                   ).then_inc(sem["inverse"], 1)
                    after(dve, "inverse", i + 1)
                    dve.tensor_copy(den_rows, recip_den[:, :, :, None].to_broadcast([P, QW // P, 4, S])
                                    ).then_inc(sem["rden"], 1)

                def normalise(i, quarter=None):
                    g, qh = i // QH, i % QH
                    n = QW if quarter is None else QW // 4
                    at = (quarter or 0) * n
                    after(dve, "spread", i + 1)
                    part = oT[:, g, qh * QW + at:qh * QW + at + n]
                    dve.tensor_tensor(part, PS[:, den_bank(i), at:at + n], part, ALU.mult).then_inc(sem["o_ready"], 1)

                def o_residual(t):
                    if t == 0:
                        after(dve, "x_res_free", 1)
                    after(dve, "oproj", t + 1)
                    dve.tensor_tensor(x_res[:, t, :], o_bank(t), x_raw[:, t, :], ALU.add
                                      ).then_inc(sem["o_res"], 1)
                    after(dve, "o_res", t + 1)
                    ins = tile_stats(x_res, t)
                    if t in (TH - 1, T - 1):
                        step(ins)

                def general_weights(g):
                    def body(qh, kt, j):
                        take(dve, "products")
                        dve.tensor_copy(g_k, one_minus[:, 1, g, bass.ds(kt, 1), j])
                        dve.tensor_copy(g_v, v_aug[:, bass.ds(kt, 1), 4 * g + j, :].rearrange("p a s -> p (a s)"))
                        dve.drain()
                        dve.tensor_scalar(g_denom, PS[:, 1, :], g_k, DENOM_MIN, ALU.mult, ALU.max)
                        dve.drain()
                        dve.reciprocal(g_over, g_denom)
                        dve.drain()
                        dve.scalar_tensor_tensor(g_u, PS[:, 0, :], 0.0, g_over, ALU.max, ALU.mult
                                                 ).then_inc(hand["u"], 1)
                        take(dve, "roots")
                        dve.tensor_tensor(g_root, g_root, g_root2, ALU.mult)
                        dve.drain()
                        dve.scalar_tensor_tensor(g_root, g_u, 1.0, g_root, ALU.add, ALU.add)
                        dve.drain()
                        dve.reciprocal(g_weight, g_root).then_inc(hand["weights"], 1)
                        take(dve, "sums")
                        rows = slice(j * S, (j + 1) * S)
                        total = g_sums[rows, g, bass.ds(qh * QW, QW)]
                        dve.tensor_tensor(total, PS[rows, 6, :], total, ALU.add).then_inc(hand["start"], 1)
                    return body

                steps_before = steps[0]
                fast = load_flag(dve)
                with dve.If(fast == 1):
                    for q in range(QUADS):
                        after(dve, "sc_dve", q + 1)
                        if q >= NBUF:
                            after(dve, "pv", q - NBUF + 1)
                        n = squared_by_scalar(q)
                        dve.tensor_scalar(root[:, q % NBUF, n * QW:4 * QW],
                                          PS[:, 2 + n:6, :].rearrange("p j q -> p (j q)"), 0.0, 1.0, ALU.max, ALU.add
                                          ).then_inc(sem["z_out"], 1)
                        if n == 1:
                            after(dve, "z_out", q + 1)
                            zt = root[:, q % NBUF, QW:2 * QW]
                            dve.tensor_tensor(zt, zt, zt, ALU.mult).then_inc(sem["z_sq_dve"], 1)
                        at, g = q % (QH * T), q // (QH * T)
                        prev = g * QH - 2
                        if q >= T and q % T == LAG - 1:
                            acc_out(q // T - 1)
                        if g:
                            if at in (1, LAG + 1):
                                recip(prev + (at > 1))
                            if at in (3, LAG + 3):
                                normalise(prev + (at > 3))
                        if g == G - 1:
                            if at == T + LAG + 1:
                                recip(LAST_SUMS - 1)
                            if at == T + LAG + 3:
                                normalise(LAST_SUMS - 1)
                            if at == T + LAG + 4:
                                o_residual(0)
                        if g + 1 < G:
                            for when, make in ((0, high_q), (3, high_k), (5, less_high), (6, middle), (7, low)):
                                if at == when:
                                    make(g + 1)
                            if at >= 8:
                                operand_out(g + 1, at - 8)
                    for t in range(1, TH - 1):
                        o_residual(t)
                    acc_out(LAST_SUMS)
                with dve.Else():
                    steps_fast, steps[0] = steps[0], steps_before
                    columns = ident[:, :].rearrange("p (j s) -> p j s", j=4)
                    dve.tensor_tensor(one_minus_q, columns[:, :, D + 1, None].to_broadcast([P, 4, P]),
                                      columns[:, :, D, None].to_broadcast([P, 4, P]), ALU.subtract)
                    dve.memset(g_sums, 0.0)
                    dve.drain().then_inc(hand["start"], 1)
                    for g in range(G):
                        if g:
                            high_q(g)
                            high_k(g)
                            less_high(g)
                            middle(g)
                            low(g)
                            for e in range(8):
                                operand_out(g, e)
                        every_key_tile(dve, general_weights(g))
                    dve.drain()
                    dve.tensor_copy(oT[:, :, :], g_sums)
                    dve.drain().then_inc(sem["acc_out"], G * QH)
                    for i in range(LAST_SUMS):
                        recip(i)
                        normalise(i)
                    for t in range(TH - 1):
                        o_residual(t)
                    assert steps[0] == steps_fast

                recip(LAST_SUMS)
                o_residual(TH - 1)
                norm_aggregate("stats", 0, 0, TH)
                for quarter in range(4):
                    normalise(LAST_SUMS, quarter)
                    if quarter == 1:
                        norm_apply(x_res, ("std", "xhat"), 0, 0, None, 0, TH)
                for t in range(TH, T):
                    o_residual(t)
                layer_norm(x_res, ("stats", "std", "xhat"), i=1, t0=TH)
                def sc(t):
                    return PS[:, 0:4, 0:4 * NK].rearrange("p c (h k) -> p c h k", h=4)

                def x_sum(t):
                    after(dve, "xexp", t + 1)
                    pr = prob[:, t % 3, :].rearrange("p (h k) -> p h k", h=H)
                    dve.tensor_reduce(psumr[:, t % 2, :], pr, AX, ALU.add).then_inc(sem["xsum"], 1)
                    after(dve, "xsum", t + 1)
                    dve.reciprocal(pinv[:, t % 2, :], psumr[:, t % 2, :]).then_inc(sem["xinv"], 1)
                    after(dve, "xinv", t + 1)
                    dve.tensor_tensor(pr, pr, pinv[:, t % 2, :, None].to_broadcast([P, H, NK]), ALU.mult
                                      ).then_inc(sem["xnorm"], 1)

                def x_residual(t):
                    after(dve, "xo", t + 1)
                    if t == 0:
                        after(dve, "bo_added", 1)
                    dve.tensor_tensor(x_res[:, t, :], PS[:, 6 + t % 2, 0:C], x_res[:, t, :], ALU.add
                                      ).then_inc(sem["x_res"], 1)
                    after(dve, "x_res", t + 1)
                    return tile_stats(x_res, t)

                for t in range(T):
                    after(dve, "xsc", t + 1)
                    dve.tensor_reduce(pmax[:, t % 2, :].rearrange("p (c h) -> p c h", c=4), sc(t), AX, ALU.max
                                      ).then_inc(sem["xmax"], 1)
                    after(dve, "xmax", t + 1)
                    if t >= 3:
                        after(dve, "ptr", 3 * (t - 2))
                    dve.tensor_tensor(prob[:, t % 3, :].rearrange("p (c h k) -> p c h k", c=4, h=4), sc(t),
                                      pmax[:, t % 2, :].rearrange("p (c h) -> p c h", c=4)[:, :, :, None]
                                      .to_broadcast([P, 4, 4, NK]), ALU.subtract).then_inc(sem["shifted"], 1)
                    if t >= 3:
                        x_residual(t - 3)
                    if nxt is not None and t >= T // 2:
                        front_stats(range(2 * (t - T // 2), 2 * (t - T // 2) + 2))
                    x_sum(t)
                x_residual(T - 3)
                if nxt is not None:
                    front_norm(("tr", T))
                x_residual(T - 2)
                step(x_residual(T - 1))
                layer_norm(x_res, ("stats", "std", "xhat"), i=2,
                           x_hat_free=("tr", T) if nxt is None else ("f_tr", T))
                if nxt is not None:
                    front_v_out(0)
                    front_v_out(1)
                for half in range(2):
                    after(dve, "xt", T + (half + 1) * TH)
                    dve.tensor_reduce(xsum[:, half, :], xT[:, :, half * N // 2:(half + 1) * N // 2], AX, ALU.add
                                      ).then_inc(sem["xs"], 1)
                after(dve, "rsc", 1)
                step(dve.scalar_tensor_tensor(route_s[:, :], PS[0:1, 7, 0:E], 1.0 / N, br_sb[:, :], ALU.mult, ALU.add))
                step(dve.max(route_m[:, :], route_s[:, :]))
                dve.max_index(route_i[:, :], route_m[:, :], route_s[:, :]).then_inc(sem["route"], 1)
                if nxt is not None:
                    front_features(v_done=2)
                    front_parts()
                after(dve, "b2_added", 1)
                for t in range(T):
                    if nxt is not None:
                        operand_out(0, t)
                    after(dve, "y", t + 1)
                    dve.tensor_tensor(x_res[:, t, :], PS[:, 4 + t % 2, 0:C], x_res[:, t, :], ALU.add
                                      ).then_inc(sem["y_res"], 1)
                batch_end(dve)

            dve.wait_ge(once["setup"], SETUP_STEPS)
            front_stats(range(T))
            norm_aggregate("f_stats", 1, 0, T)
            at = 0
            for n, (kind, i, st) in enumerate(SETS):
                if kind == "n":
                    at += H // 2
                    continue
                if stored_before(n, st):
                    dve.wait_ge(once[f"stored{st}"], 16 * stored_before(n, st))
                for k in range(H):
                    at += 1
                    dve.wait_ge(once["mn"], at)
                    dve.tensor_scalar(m_stage[:, :, k, :], PS[:, k % 4, 0:B * NK].rearrange("p (b k) -> p b k", b=B),
                                      float(INNER // H) ** -0.5, None, ALU.mult).then_inc(once["m_out"], 1)
            norm_apply(x_raw, ("f_std", "f_xhat"), 0, 1, None, 0, T)
            front_features()
            front_parts()
            for e in range(8):
                operand_out(0, e)
            batch_end(dve)
            all_batches(dve, batch)

        @block.tensor
        def _(pe):
            pe.wait_ge(once["setup"], SETUP_STEPS)
            pe.wait_ge(once["kv_weights"], 48)
            for c in range(2):
                for b in range(B):
                    last = pe.transpose(PS[0:CEH, 4 + c, b * NK:(b + 1) * NK], ctx_sb[:, b, c * CEH:(c + 1) * CEH],
                                        ident[0:NK, 0:NK])
                last.then_inc(once["ctx_tr"], 1)
            pe.wait_ge(once["ctx_out"], 2)
            for i in range(2 * HP):
                if i >= 4:
                    pe.wait_ge(once["kvx_out"], i - 3)
                w, hp = (Wk_sb, Wv_sb)[i // HP], i % HP
                for c in range(2):
                    last = pe.matmul(PS[:, i % 4, 0:B * NK], w[:, c, hp * P:(hp + 1) * P],
                                     ctxT[:, c].rearrange("p b k -> p (b k)"), start=(c == 0), stop=(c == 1))
                last.then_inc(once["kvx"], 1)
            pe.wait_ge(once["weights"], 16 * N_WEIGHT_DMAS)
            for i in range(4):
                for h in (2 * i, 2 * i + 1):
                    for c in range(CT):
                        last = pe.transpose(PS[:, 4 + i, (h % 2) * C + c * P:(h % 2) * C + (c + 1) * P],
                                            Wq_nat[:, c, h * P:(h + 1) * P], ident[:, :])
                last.then_inc(once["wtr"], 1)
            pe.wait_ge(once["kvx_out"], 2 * HP)
            for i in range(3):
                for c in range(CT):
                    for o in range(CT):
                        last = pe.transpose(PS[:, i, c * C + o * P:c * C + (o + 1) * P],
                                            w_nat[:, i, o, c * P:(c + 1) * P], ident[:, :])
                last.then_inc(once["wtr"], 1)
            for i in range(2):
                if i:
                    pe.wait_ge(once["wtr_out"], 1)
                for g in (2 * i, 2 * i + 1):
                    for o in range(CT):
                        last = pe.transpose(PS[:, 3 + i, (g % 2) * C + o * P:(g % 2) * C + (o + 1) * P],
                                            wo_pad[:, o, g].rearrange("p j s -> p (j s)"), ident[:, :])
                last.then_inc(once["wtr"], 1)
            pe.wait_ge(once["wtr_out"], 9)
            n_done, m_done = 0, 0
            for kind, i, st in SETS:
                if kind == "n":
                    for k in range(H // 2):
                        if n_done >= 4:
                            pe.wait_ge(once["n_out"], n_done - 3)
                        odd = k % 2
                        for h in range(2):
                            hp = 2 * (k // 2) + h
                            last = pe.matmul(PS[0:NK, 4 + k % 4, h * C:(h + 1) * C],
                                             vx[64 * odd:64 * odd + 64, hp, i, :], Wo_sb[64 * odd:64 * odd + 64, hp, :],
                                             start=True, stop=True)
                        last.then_inc(once["mn"], 1)
                        n_done += 1
                else:
                    for h in range(H):
                        if m_done >= 4:
                            pe.wait_ge(once["m_out"], m_done - 3)
                        odd = h % 2
                        pe.matmul(PS[:, h % 4, 0:B * NK], WqT[64 * odd:64 * odd + 64, h // 2, i * P:(i + 1) * P],
                                  kx[64 * odd:64 * odd + 64, h // 2].rearrange("p b k -> p (b k)"),
                                  start=True, stop=True).then_inc(once["mn"], 1)
                        m_done += 1
            pe.wait_ge(once["m_out"], 2 * H)
            pe.wait_ge(once["n_out"], B * H // 2)

            def transpose_x(i, t):
                after(pe, "xhat", i * T + t + 1)
                if i * T + t >= 2:
                    after(pe, "xt", i * T + t - 1)
                for c in range(CT):
                    last = pe.transpose(tr_bank(i, t)[:, c * P:(c + 1) * P], x_hat[:, t, c * P:(c + 1) * P], ident[:, :])
                last.then_inc(sem["tr"], 1)

            def front_transposes():
                for t in range(T):
                    after(pe, "f_xhat", t + 1)
                    if t >= 4:
                        after(pe, "f_xt", t - 3)
                    for c in range(CT):
                        last = pe.transpose(PS[:, t % 4, c * P:(c + 1) * P], x_hat[:, t, c * P:(c + 1) * P], ident[:, :])
                    last.then_inc(sem["f_tr"], 1)

            def front_qk(t):
                after(pe, "f_xt", min(T, T - 1 + t))
                if t >= 2:
                    after(pe, "qk_out", t - 1)
                for c in range(CT):
                    last = pe.matmul(PS[:, 2 + t % 2, :], xT_next[:, c, t * P:(t + 1) * P], wqkvT[:, c, 0:2 * C],
                                     start=(c == 0), stop=(c == CT - 1))
                last.then_inc(sem["qk"], 1)

            def front_v(t):
                if t >= 2:
                    after(pe, "v_out", t - 1)
                for c in range(CT):
                    last = pe.matmul(PS[:, 4 + t % 2, 0:C], xT_next[:, c, t * P:(t + 1) * P], wqkvT[:, c, 2 * C:3 * C],
                                     start=(c == 0), stop=(c == CT - 1))
                last.then_inc(sem["v"], 1)

            def front_project(tiles):
                for t in tiles:
                    front_qk(t)
                    front_v(t)

            def front_least_norm(_=0):
                after(pe, "nlow", 1)
                pe.transpose(PS[0:1, 6, 0:P], norm_low[:, :], ident[:, :]).then_inc(sem["nlowT"], 1)

            def front_turn_q(f):
                g, half = f // 2, f % 2
                if f == 0:
                    after(pe, "qk_out", T)
                    after(pe, "scaled", 1)
                    after(pe, "flag", 1)
                if f >= 2:
                    after(pe, "q_ready", f - 1)
                for i in range(T // 2):
                    last = pe.transpose(PS[:, 6 + f % 2, i * P:(i + 1) * P],
                                        feat[:, 0, g, half * T // 2 + i].rearrange("p j s -> p (j s)"), ident[:, :])
                last.then_inc(sem["trq"], 1)

            def front_gmat(g):
                if g == 0:
                    after(pe, "v_out", T)
                    after(pe, "scaled", 2)
                after(pe, "q_ready", 2 * G - 1 + g % 2) if g < 2 else after(pe, "g_ready", g - 1)
                for t in range(T):
                    last = pe.matmul(PS[:, 6 + g % 2, 0:P],
                                     feat[:, 1, g, t].rearrange("p j s -> p (j s)"),
                                     v_aug[:, t, 4 * g:4 * g + 4, :].rearrange("p h s -> p (h s)"),
                                     start=(t == 0), stop=(t == T - 1))
                last.then_inc(sem["gmat"], 1)

            def turn_operand(g, e, general=False):
                split, turned, ready, n = ("split", "tr6", "op_ready", g - 1) if g else ("f_split", "f_tr6", "f_op_ready", 0)
                if e == 0:
                    after(pe, split, 4 * n + 4)
                if n or e:
                    after(pe, ready, 8 * n + e)
                if g == 0 and e == 0:
                    after(pe, "g_ready", G)
                if n and e == 0 and not general:
                    after(pe, "o_ready", QH * n)
                for t in range(T):
                    last = pe.transpose(PS[0:KR, 7, :].bitcast(BF16)[:, t * P:(t + 1) * P],
                                        parts[:, e // 4, 4 * t + e % 4].rearrange("p s f -> p (s f)"), ident16[:, :])
                last.then_inc(sem[turned], 1)

            def batch(b, nxt):
                def scores(q):
                    g, qh, kt = q // (QH * T), q // T % QH, q % T
                    if q >= 2:
                        after(pe, "squared", q - 1)
                        if squared_by_scalar(q - 2) == 1:
                            after(pe, "z_out", q - 1)
                    if g and q % (QH * T) == 0:
                        after(pe, "op_ready", 8 * g)
                    for j in range(4):
                        if j == 2 and q >= 1:
                            after(pe, "z_out", q)
                        bank = 2 * (q % 2) + j if j < 2 else 2 + j
                        mm = pe.matmul(PS[:, bank, :], opT[g % 2][0:KR, 1, j, kt * P:(kt + 1) * P],
                                       opT[g % 2][0:KR, 0, j, qh * QW:(qh + 1) * QW], start=True, stop=True)
                        if j == squared_by_scalar(q) - 1:
                            mm.then_inc(sem["sc_act"], 1)
                        if j == 3:
                            mm.then_inc(sem["sc_dve"], 1)

                def weigh(q):
                    g, qh, kt = q // (QH * T), q // T % QH, q % T
                    i = q // T
                    acc = PS[:, 6, :]
                    if kt == 0:
                        if i >= 1:
                            after(pe, "acc_out", i)
                        pe.matmul(acc, Gm[:, g, :], qT[:, g, qh * QW:(qh + 1) * QW], start=True, stop=False,
                                  skip_group_check=True)
                    after(pe, "rooted", q + 1)
                    for j in range(4):
                        mm = pe.matmul(acc[j * S:(j + 1) * S, :], v_aug[:, kt, 4 * g + j, :],
                                       root[:, q % NBUF, j * QW:(j + 1) * QW], start=False, stop=(kt == T - 1),
                                       skip_group_check=True)
                    mm.then_inc(sem["pv"], 1)

                def denominators(i):
                    g, qh = i // QH, i % QH
                    after(pe, "acc_out", i + 1)
                    if i:
                        after(pe, "o_ready", i)
                    after(pe, "op_ready", 8 * min(G - 1, i // QH + 1))
                    for t in range(QW // P):
                        last = pe.matmul(PS[:, den_bank(i), 4 * t:4 * t + 4], oT[:, g, qh * QW + t * P:qh * QW + (t + 1) * P],
                                         den_pick[:, 0:P:S], start=True, stop=True)
                    last.then_inc(sem["den"], 1)

                def spread(i):
                    after(pe, "rden", i + 1)
                    for t in range(QW // P):
                        last = pe.matmul(PS[:, den_bank(i), t * P:(t + 1) * P],
                                         den_rows[:, t].rearrange("p j s -> p (j s)"), ident[:, :],
                                         start=True, stop=True)
                    last.then_inc(sem["spread"], 1)

                def o_project(t):
                    after(pe, "o_ready", LAST_SUMS + (t - TH + 1 if t >= TH else 0))
                    if t:
                        after(pe, "o_res", t if t < TH else t - 1)
                    for g in range(G):
                        last = pe.matmul(o_bank(t), oT[:, g, t * P:(t + 1) * P], woT[:, g, :],
                                         start=(g == 0), stop=(g == G - 1))
                    last.then_inc(sem["oproj"], 1)

                def general_products(g):
                    def body(qh, kt, j):
                        take(pe, "start")
                        pe.matmul(PS[:, 0, :], opT[g % 2][0:KR, 1, j, bass.ds(kt * P, P)],
                                  opT[g % 2][0:KR, 0, j, bass.ds(qh * QW, QW)], start=True, stop=True)
                        pe.matmul(PS[:, 1, :], one_minus_q[:, j, :], qT[:, g, bass.ds(qh * QW, QW)],
                                  start=True, stop=True).then_inc(hand["products"], 1)
                        take(pe, "weights")
                        pe.matmul(PS[j * S:(j + 1) * S, 6, :], g_v, g_weight, start=True, stop=True
                                  ).then_inc(hand["sums"], 1)
                    return body

                fast = load_flag(pe)
                with pe.If(fast == 1):
                    for q in range(QUADS + LAG):
                        if q < QUADS:
                            scores(q)
                        if q >= LAG:
                            weigh(q - LAG)
                        at, gq = q % (QH * T), q // (QH * T)
                        if 0 < gq < G and at in (0, LAG):
                            denominators(gq * QH - 2 + (at > 0))
                        if 0 < gq < G and at in (2, LAG + 2):
                            spread(gq * QH - 2 + (at > 2))
                        if gq + 1 < G and at >= 8:
                            turn_operand(gq + 1, at - 8)
                        if q == QUADS - T + LAG:
                            denominators(LAST_SUMS - 1)
                        if q == QUADS - T + LAG + 2:
                            spread(LAST_SUMS - 1)
                        if QUADS - 1 <= q < QUADS + TH - 2:
                            o_project(q - (QUADS - 1))
                    after(pe, "squared", QUADS)
                    after(pe, "z_out", QUADS)
                with pe.Else():
                    for g in range(G):
                        if g:
                            for e in range(8):
                                turn_operand(g, e, general=True)
                            after(pe, "op_ready", 8 * g)
                        every_key_tile(pe, general_products(g))
                    take(pe, "start")
                    for i in range(LAST_SUMS):
                        denominators(i)
                        spread(i)
                    for t in range(TH - 1):
                        o_project(t)

                denominators(LAST_SUMS)
                o_project(TH - 1)
                spread(LAST_SUMS)
                o_project(TH)
                o_project(TH + 1)
                for t in range(TH):
                    transpose_x(0, t)
                for t in range(TH + 2, T):
                    o_project(t)

                def x_scores(t):
                    if t >= 1:
                        after(pe, "shifted", t)
                    for i in range(4):
                        for c in range(CT):
                            last = pe.matmul(PS[:, i, 0:4 * NK], xT[:, c, t * P:(t + 1) * P],
                                             Mb[:, c, 4 * i * NK:4 * (i + 1) * NK],
                                             start=(c == 0), stop=(c == CT - 1))
                    last.then_inc(sem["xsc"], 1)

                def x_turn(t):
                    after(pe, "xnorm", t + 1)
                    for i in range(3):
                        if 3 * t + i >= 2:
                            after(pe, "pt_out", 3 * t + i - 1)
                        for k in range(4 * i, min(4 * i + 4, PT)):
                            n = P if k < PT - 1 else LAST
                            last = pe.transpose(PS[0:n, 4 + (3 * t + i) % 2, (k % 4) * P:(k % 4 + 1) * P],
                                                prob[:, t % 3, k * P:k * P + n], ident[:, :])
                        last.then_inc(sem["ptr"], 1)

                def x_weigh(t):
                    if t == 0:
                        after(pe, "mn_in", 48)
                    after(pe, "pt_out", 3 * t + 3)
                    if t >= 2:
                        after(pe, "x_res", t - 1)
                    for k in range(PT):
                        n = P if k < PT - 1 else LAST
                        last = pe.matmul(PS[:, 6 + t % 2, 0:C], pT[0:n, t % 2, k, :], Nb[0:n, k, :],
                                         start=(k == 0), stop=(k == PT - 1))
                    last.then_inc(sem["xo"], 1)

                after(pe, "xt", TH)
                after(pe, "mn_in", 48)
                for t in range(T + 2):
                    if t < T:
                        x_scores(t)
                    if t == 0:
                        for rest_t in range(TH, T):
                            transpose_x(0, rest_t)
                        after(pe, "xt", T)
                    if t == T:
                        x_weigh(t - 2)
                    if 1 <= t <= T:
                        x_turn(t - 1)
                    if t >= 2 and t != T:
                        x_weigh(t - 2)
                after(pe, "shifted", T)
                after(pe, "pt_out", 3 * T)
                if nxt is not None:
                    front_transposes()
                    front_project(range(2))
                    after(pe, "f_xt", T)
                for t in range(T):
                    transpose_x(1, t)
                if nxt is not None:
                    front_project(range(2, 3))
                after(pe, "xs", 2)
                for half in range(2):
                    for c in range(CT):
                        last = pe.matmul(PS[0:1, 7, 0:E], xsum[:, half, c:c + 1], Wr_sb[:, c, :],
                                         start=(half == 0 and c == 0), stop=(half == 1 and c == CT - 1))
                last.then_inc(sem["rsc"], 1)
                if nxt is not None:
                    front_project(range(3, T))
                after(pe, "xt", 2 * T)
                after(pe, "w1_in", PER["w1_in"])
                pe.transpose(PS[:, 7, 0:FT], b1_rows[:, :], ident[0:FT, 0:FT]).then_inc(sem["b1_tr"], 1)
                if nxt is not None:
                    after(pe, "qk_out", T)
                    after(pe, "b1_out", 1)
                for f in range(2 * FT):
                    ft, half = f // 2, f % 2
                    if f >= 4:
                        after(pe, "h_out", f - 3)
                    for c in range(CT):
                        last = pe.matmul(PS[:, f % 4, :], W1_sb[:, c, ft * P:(ft + 1) * P],
                                         xT[:, c, half * 512:(half + 1) * 512], start=(c == 0), stop=(c == CT - 1))
                    last.then_inc(sem["h_prod"], 1)
                    if nxt is not None:
                        for kind, i in SIDE.get(f, ()):
                            {"low": front_least_norm, "qT": front_turn_q, "Gm": front_gmat}[kind](i)
                if nxt is not None:
                    after(pe, "v_out", T)
                after(pe, "w2_in", PER["w2_in"])
                after(pe, "h_out", 2 * FT)
                for t in range(T):
                    if nxt is not None:
                        turn_operand(0, t)
                    if t >= 2:
                        after(pe, "y_res", t - 1)
                    for f in range(FT):
                        last = pe.matmul(PS[:, 4 + t % 2, 0:C], hT[:, f, t * P:(t + 1) * P], W2_sb[:, f, :],
                                         start=(f == 0), stop=(f == FT - 1))
                    last.then_inc(sem["y"], 1)
                batch_end(pe)

            front_transposes()
            front_project(range(T))
            front_least_norm()
            for f in range(2 * G):
                front_turn_q(f)
            for g in range(G):
                front_gmat(g)
            for e in range(8):
                turn_operand(0, e)
            batch_end(pe)
            all_batches(pe, batch)


_INS = ['x', 'ctx_768', 'L0_attn_wq', 'L0_attn_wk', 'L0_attn_wv', 'L0_attn_wo', 'L0_xattn_Wq', 'L0_xattn_Wk',
        'L0_xattn_Wv', 'L0_xattn_Wo', 'L0_xattn_bo', 'L0_ffn_Wr', 'L0_ffn_br', 'L0_ffn_W1', 'L0_ffn_b1',
        'L0_ffn_W2', 'L0_ffn_b2']
_OUTS = [((4, 1024, 256), 'float32')]


def kernel(**inputs):
    import numpy as _np
    import concourse.bacc as _bacc
    from concourse import mybir as _mybir
    from concourse.bass_utils import run_bass_kernel_spmd as _run

    nc = _bacc.Bacc("TRN2", target_bir_lowering=False, num_devices=1)
    arrays, args = {}, []
    for name in _INS:
        a = _np.ascontiguousarray(inputs[name])
        arrays[f"in_{name}_dram"] = a
        args.append(nc.dram_tensor(f"in_{name}_dram", a.shape, _mybir.dt.from_np(a.dtype), kind="ExternalInput").ap())
    for i, (shape, dtype) in enumerate(_OUTS):
        dt = _mybir.dt.from_np(_np.dtype(dtype))
        args.append(nc.dram_tensor(f"out_{i}_dram", shape, dt, kind="ExternalOutput").ap())
    decoder_layer(nc, *args)
    r = _run(nc, [arrays], core_ids=[0])
    return r.results[0]["out_0_dram"]
```
